# Optimizing a Trainium2 kernel written in Bass

```python
import numpy as np
import jax
import jax.numpy as jnp

def _softmax(x, axis=-1):
    return jax.nn.softmax(x, axis=axis)

def _gelu(x):
    return jax.nn.gelu(x, approximate=True)

def _silu(x):
    return jax.nn.silu(x)

def _sigmoid(x):
    return jax.nn.sigmoid(x)

def _layernorm(x, axis=-1, eps=1e-05):
    m = jnp.mean(x, axis=axis, keepdims=True)
    v = jnp.var(x, axis=axis, keepdims=True)
    return (x - m) / jnp.sqrt(v + eps)

def _scatter_add(tgt, idx, src, axis=0):
    return tgt.at[idx].add(src)

def _segment_sum(src, seg, n):
    return jax.ops.segment_sum(src, seg, n)
kernel_name = 'mk_gnn_resnorm_d4_gnn_r8_3999c7'

def setup_inputs(seed: int=0):
    np.random.seed(seed)
    _w = jnp.asarray

    def _rec_inputs():
        import jax
        import jax.numpy as jnp
        _gk = jax.random.key(seed)
        x = -0.0001006 + 1 * jax.random.normal(jax.random.fold_in(_gk, 1), (6250, 96), jnp.float32)
        _s = jax.random.randint(jax.random.fold_in(_gk, 2), (50000,), 0, 6250, jnp.int32)
        _d = jax.random.randint(jax.random.fold_in(_gk, 3), (50000,), 0, 6250, jnp.int32)
        _loop = jnp.arange(6250, dtype=jnp.int32)
        src = jnp.concatenate([_s, _d, _loop])
        dst = jnp.concatenate([_d, _s, _loop])
        _o = jnp.argsort(dst, stable=True)
        src = src[_o]
        dst = dst[_o]
        edge_attr_17 = jax.random.uniform(jax.random.fold_in(_gk, 11), (106250, 17), jnp.float32, 0.0, 1)
        edge_attr_32 = 0.000196303 + 1.00016 * jax.random.normal(jax.random.fold_in(_gk, 12), (106250, 32), jnp.float32)
        return (x, src, dst, edge_attr_17, edge_attr_32)
    x, src, dst, edge_attr_17, edge_attr_32 = _rec_inputs()

    def _L0_gnn_setup():
        import jax, jax.numpy as jnp
        import numpy as np
        N = 6250
        E = 100000
        D = 96
        ED = 17
        key = jax.random.key(seed)
        ks = jax.random.split(key, 12)
        x = jax.random.normal(ks[0], (N, D), dtype=jnp.float32)
        edge_index = jax.random.randint(ks[1], (2, E), 0, N, dtype=jnp.int64)
        edge_attr = jax.random.uniform(ks[2], (E, ED), dtype=jnp.float32)
        s = 1.0 / np.sqrt(ED)
        W1 = jax.random.uniform(ks[3], (D, ED), jnp.float32, -s, s)
        b1 = jax.random.uniform(ks[4], (D,), jnp.float32, -s, s)
        s = 1.0 / np.sqrt(D)
        W2 = jax.random.uniform(ks[5], (D, D), jnp.float32, -s, s)
        b2 = jax.random.uniform(ks[6], (D,), jnp.float32, -s, s)
        Ws = jax.random.uniform(ks[7], (D, D), jnp.float32, -s, s)
        bs = jax.random.uniform(ks[8], (D,), jnp.float32, -s, s)
        Wn = jax.random.uniform(ks[9], (D, D), jnp.float32, -s, s)
        bn = jax.random.uniform(ks[10], (D,), jnp.float32, -s, s)
        return {'x': x, 'edge_index': edge_index, 'edge_attr': edge_attr, 'W1': W1, 'b1': b1, 'W2': W2, 'b2': b2, 'Ws': Ws, 'bs': bs, 'Wn': Wn, 'bn': bn}
    _L0_gnn_all = _L0_gnn_setup()
    _L0_gnn_in = {k: v for k, v in _L0_gnn_all.items() if k in ('W1', 'b1', 'W2', 'b2', 'Ws', 'bs', 'Wn', 'bn')}
    del _L0_gnn_all

    def _L1_gnn_setup():
        import jax, jax.numpy as jnp
        import numpy as np
        EPS = 1e-05

        def _gcn_conv(x, edge_index, W, b):
            h = x @ W
            src, dst = (edge_index[0], edge_index[1])
            msgs = h[src]
            agg = jax.ops.segment_sum(msgs, dst, num_segments=x.shape[0])
            return agg + b

        def _graph_norm(x, weight, bias, mean_scale):
            mean = jnp.mean(x, axis=0, keepdims=True)
            xc = x - mean_scale * mean
            var = jnp.mean(xc * xc, axis=0, keepdims=True)
            return xc * jax.lax.rsqrt(var + EPS) * weight + bias
        key = jax.random.key(seed)
        ks = jax.random.split(key, 8)
        N, E, D = (6250, 100000, 96)
        x = jax.random.normal(ks[0], (N, D), dtype=jnp.float32)
        edge_index = jax.random.randint(ks[1], (2, E), 0, N, dtype=jnp.int32)
        s = 1.0 / np.sqrt(D)
        W1 = jax.random.normal(ks[2], (D, D), dtype=jnp.float32) * s
        b1 = jnp.zeros((D,), dtype=jnp.float32)
        W2 = jax.random.normal(ks[3], (D, D), dtype=jnp.float32) * s
        b2 = jnp.zeros((D,), dtype=jnp.float32)
        gn1_w = jnp.ones((D,), dtype=jnp.float32)
        gn1_b = jnp.zeros((D,), dtype=jnp.float32)
        gn1_a = jnp.ones((D,), dtype=jnp.float32)
        gn2_w = jnp.ones((D,), dtype=jnp.float32)
        gn2_b = jnp.zeros((D,), dtype=jnp.float32)
        gn2_a = jnp.ones((D,), dtype=jnp.float32)
        return {'x': x, 'edge_index': edge_index, 'W1': W1, 'b1': b1, 'W2': W2, 'b2': b2, 'gn1_w': gn1_w, 'gn1_b': gn1_b, 'gn1_a': gn1_a, 'gn2_w': gn2_w, 'gn2_b': gn2_b, 'gn2_a': gn2_a}
    _L1_gnn_all = _L1_gnn_setup()
    _L1_gnn_in = {k: v for k, v in _L1_gnn_all.items() if k in ('W1', 'b1', 'W2', 'b2', 'gn1_w', 'gn1_b', 'gn1_a', 'gn2_w', 'gn2_b', 'gn2_a')}
    del _L1_gnn_all

    def _L2_gnn_setup():
        import jax, jax.numpy as jnp
        import numpy as np
        N, E = (6250, 100000)
        DIN = DOUT = 96
        DE = 32

        def _egnn_conv(x, src, dst, edge_attr, W_msg, W_edge, W_root, b):
            msg = x[src] @ W_msg + edge_attr @ W_edge
            agg = jax.ops.segment_max(msg, dst, num_segments=x.shape[0])
            agg = jnp.where(jnp.isneginf(agg), 0.0, agg)
            return agg + x @ W_root + b
        key = jax.random.key(seed)
        ks = jax.random.split(key, 10)
        rn = lambda k, sh, sc: jax.random.normal(k, sh, jnp.float32) * sc
        return {'X': rn(ks[0], (N, DIN), 1.0), 'edge_index': jax.random.randint(ks[1], (2, E), 0, N, jnp.int32), 'edge_attr': rn(ks[2], (E, DE), 1.0), 'W1_msg': rn(ks[3], (DIN, DOUT), DIN ** (-0.5)), 'W1_edge': rn(ks[4], (DE, DOUT), DE ** (-0.5)), 'W1_root': rn(ks[5], (DIN, DOUT), DIN ** (-0.5)), 'b1': jnp.zeros((DOUT,), jnp.float32), 'W2_msg': rn(ks[6], (DOUT, DOUT), DOUT ** (-0.5)), 'W2_edge': rn(ks[7], (DE, DOUT), DE ** (-0.5)), 'W2_root': rn(ks[8], (DOUT, DOUT), DOUT ** (-0.5)), 'b2': jnp.zeros((DOUT,), jnp.float32)}
    _L2_gnn_all = _L2_gnn_setup()
    _L2_gnn_in = {k: v for k, v in _L2_gnn_all.items() if k in ('W1_msg', 'W1_edge', 'W1_root', 'b1', 'W2_msg', 'W2_edge', 'W2_root', 'b2')}
    del _L2_gnn_all

    def _L3_gnn_setup():
        import jax, jax.numpy as jnp
        import numpy as np
        N_NODES = 6250
        N_EDGES = 100000
        D_IN = 96
        D_OUT = 96
        key = jax.random.key(seed)
        k1, k2, k3, k4, k5, k6 = jax.random.split(key, 6)
        x = jax.random.normal(k1, (N_NODES, D_IN), dtype=jnp.float32)
        edge_index = jax.random.randint(k2, (2, N_EDGES), 0, N_NODES, dtype=jnp.int32)
        W_lin = jax.random.normal(k3, (D_OUT, D_IN), dtype=jnp.float32) * 0.1
        b_lin = jax.random.normal(k4, (D_OUT,), dtype=jnp.float32) * 0.1
        W_root = jax.random.normal(k5, (D_OUT, D_IN), dtype=jnp.float32) * 0.1
        b_root = jax.random.normal(k6, (D_OUT,), dtype=jnp.float32) * 0.1
        return {'x': x, 'edge_index': edge_index, 'W_lin': W_lin, 'b_lin': b_lin, 'W_root': W_root, 'b_root': b_root}
    _L3_gnn_all = _L3_gnn_setup()
    _L3_gnn_in = {k: v for k, v in _L3_gnn_all.items() if k in ('W_lin', 'b_lin', 'W_root', 'b_root')}
    del _L3_gnn_all
    return {'x': x, 'src': src, 'dst': dst, 'edge_attr_17': edge_attr_17, 'edge_attr_32': edge_attr_32, 'L0_gnn_W1': _L0_gnn_in['W1'], 'L0_gnn_b1': _L0_gnn_in['b1'], 'L0_gnn_W2': _L0_gnn_in['W2'], 'L0_gnn_b2': _L0_gnn_in['b2'], 'L0_gnn_Ws': _L0_gnn_in['Ws'], 'L0_gnn_bs': _L0_gnn_in['bs'], 'L0_gnn_Wn': _L0_gnn_in['Wn'], 'L0_gnn_bn': _L0_gnn_in['bn'], 'L1_gnn_W1': _L1_gnn_in['W1'], 'L1_gnn_b1': _L1_gnn_in['b1'], 'L1_gnn_W2': _L1_gnn_in['W2'], 'L1_gnn_b2': _L1_gnn_in['b2'], 'L1_gnn_gn1_w': _L1_gnn_in['gn1_w'], 'L1_gnn_gn1_b': _L1_gnn_in['gn1_b'], 'L1_gnn_gn1_a': _L1_gnn_in['gn1_a'], 'L1_gnn_gn2_w': _L1_gnn_in['gn2_w'], 'L1_gnn_gn2_b': _L1_gnn_in['gn2_b'], 'L1_gnn_gn2_a': _L1_gnn_in['gn2_a'], 'L2_gnn_W1_msg': _L2_gnn_in['W1_msg'], 'L2_gnn_W1_edge': _L2_gnn_in['W1_edge'], 'L2_gnn_W1_root': _L2_gnn_in['W1_root'], 'L2_gnn_b1': _L2_gnn_in['b1'], 'L2_gnn_W2_msg': _L2_gnn_in['W2_msg'], 'L2_gnn_W2_edge': _L2_gnn_in['W2_edge'], 'L2_gnn_W2_root': _L2_gnn_in['W2_root'], 'L2_gnn_b2': _L2_gnn_in['b2'], 'L3_gnn_W_lin': _L3_gnn_in['W_lin'], 'L3_gnn_b_lin': _L3_gnn_in['b_lin'], 'L3_gnn_W_root': _L3_gnn_in['W_root'], 'L3_gnn_b_root': _L3_gnn_in['b_root']}

def reference(x, src, dst, edge_attr_17, edge_attr_32, L0_gnn_W1, L0_gnn_b1, L0_gnn_W2, L0_gnn_b2, L0_gnn_Ws, L0_gnn_bs, L0_gnn_Wn, L0_gnn_bn, L1_gnn_W1, L1_gnn_b1, L1_gnn_W2, L1_gnn_b2, L1_gnn_gn1_w, L1_gnn_gn1_b, L1_gnn_gn1_a, L1_gnn_gn2_w, L1_gnn_gn2_b, L1_gnn_gn2_a, L2_gnn_W1_msg, L2_gnn_W1_edge, L2_gnn_W1_root, L2_gnn_b1, L2_gnn_W2_msg, L2_gnn_W2_edge, L2_gnn_W2_root, L2_gnn_b2, L3_gnn_W_lin, L3_gnn_b_lin, L3_gnn_W_root, L3_gnn_b_root):
    import jax
    import jax.numpy as jnp

    def _L0_gnn_ref(x, edge_index, edge_attr, W1, b1, W2, b2, Ws, bs, Wn, bn):
        import jax, jax.numpy as jnp
        import numpy as np
        N = 6250
        E = 100000
        D = 96
        ED = 17
        src, dst = (edge_index[0], edge_index[1])
        h = jax.nn.relu(edge_attr @ W1.T + b1)
        w = h @ W2.T + b2
        msg = w * x[src]
        agg = jax.ops.segment_sum(msg, dst, num_segments=x.shape[0])
        return jax.nn.relu(x @ Ws.T + bs + agg @ Wn.T + bn)

    def _L1_gnn_ref(x, edge_index, W1, b1, W2, b2, gn1_w, gn1_b, gn1_a, gn2_w, gn2_b, gn2_a):
        import jax, jax.numpy as jnp
        import numpy as np
        EPS = 1e-05

        def _gcn_conv(x, edge_index, W, b):
            h = x @ W
            src, dst = (edge_index[0], edge_index[1])
            msgs = h[src]
            agg = jax.ops.segment_sum(msgs, dst, num_segments=x.shape[0])
            return agg + b

        def _graph_norm(x, weight, bias, mean_scale):
            mean = jnp.mean(x, axis=0, keepdims=True)
            xc = x - mean_scale * mean
            var = jnp.mean(xc * xc, axis=0, keepdims=True)
            return xc * jax.lax.rsqrt(var + EPS) * weight + bias
        identity = x
        h = _gcn_conv(x, edge_index, W1, b1)
        h = _graph_norm(h, gn1_w, gn1_b, gn1_a)
        h = jax.nn.relu(h)
        h = h + identity
        identity = h
        h2 = _gcn_conv(h, edge_index, W2, b2)
        h2 = _graph_norm(h2, gn2_w, gn2_b, gn2_a)
        h2 = jax.nn.relu(h2)
        h2 = h2 + identity
        return h2

    def _L2_gnn_ref(X, edge_index, edge_attr, W1_msg, W1_edge, W1_root, b1, W2_msg, W2_edge, W2_root, b2):
        import jax, jax.numpy as jnp
        import numpy as np
        N, E = (6250, 100000)
        DIN = DOUT = 96
        DE = 32

        def _egnn_conv(x, src, dst, edge_attr, W_msg, W_edge, W_root, b):
            msg = x[src] @ W_msg + edge_attr @ W_edge
            agg = jax.ops.segment_max(msg, dst, num_segments=x.shape[0])
            agg = jnp.where(jnp.isneginf(agg), 0.0, agg)
            return agg + x @ W_root + b
        src, dst = (edge_index[0], edge_index[1])
        c1 = jax.nn.leaky_relu(_egnn_conv(X, src, dst, edge_attr, W1_msg, W1_edge, W1_root, b1))
        c2 = jax.nn.leaky_relu(_egnn_conv(c1, src, dst, edge_attr, W2_msg, W2_edge, W2_root, b2))
        return c2

    def _L3_gnn_ref(x, edge_index, W_lin, b_lin, W_root, b_root):
        import jax, jax.numpy as jnp
        import numpy as np
        N_NODES = 6250
        N_EDGES = 100000
        D_IN = 96
        D_OUT = 96
        src, dst = (edge_index[0], edge_index[1])
        n = x.shape[0]
        deg = jax.ops.segment_sum(jnp.ones(src.shape[0], dtype=x.dtype), dst, num_segments=n)
        dinv = jax.lax.rsqrt(jnp.maximum(deg, 1.0))
        norm = dinv[src] * dinv[dst]
        h = x @ W_lin.T + b_lin
        msgs = h[src] * norm[:, None]
        agg = jax.ops.segment_sum(msgs, dst, num_segments=n)
        out = agg + x @ W_root.T + b_root
        return jax.nn.relu(out)
    edge_index = jnp.stack([src, dst])
    x = _layernorm(x + _L0_gnn_ref(x, edge_index, edge_attr_17, L0_gnn_W1, L0_gnn_b1, L0_gnn_W2, L0_gnn_b2, L0_gnn_Ws, L0_gnn_bs, L0_gnn_Wn, L0_gnn_bn), axis=-1)
    x = _layernorm(x + _L1_gnn_ref(x, edge_index, L1_gnn_W1, L1_gnn_b1, L1_gnn_W2, L1_gnn_b2, L1_gnn_gn1_w, L1_gnn_gn1_b, L1_gnn_gn1_a, L1_gnn_gn2_w, L1_gnn_gn2_b, L1_gnn_gn2_a), axis=-1)
    x = _layernorm(x + _L2_gnn_ref(x, edge_index, edge_attr_32, L2_gnn_W1_msg, L2_gnn_W1_edge, L2_gnn_W1_root, L2_gnn_b1, L2_gnn_W2_msg, L2_gnn_W2_edge, L2_gnn_W2_root, L2_gnn_b2), axis=-1)
    x = _layernorm(x + _L3_gnn_ref(x, edge_index, L3_gnn_W_lin, L3_gnn_b_lin, L3_gnn_W_root, L3_gnn_b_root), axis=-1)
    return x

_drawn_inputs = setup_inputs


def setup_inputs(seed=0):
    import zlib

    import numpy as np

    out = dict(_drawn_inputs(seed))
    spreads = {'L1_gnn_b1': (0.0, 0.8),
     'L1_gnn_b2': (0.0, 0.8),
     'L1_gnn_gn1_w': (1.0, 0.2),
     'L1_gnn_gn1_b': (0.0, 0.353),
     'L1_gnn_gn1_a': (1.0, 0.6),
     'L1_gnn_gn2_w': (1.0, 0.2),
     'L1_gnn_gn2_b': (0.0, 0.373),
     'L1_gnn_gn2_a': (1.0, 0.2),
     'L2_gnn_b1': (0.0, 0.1),
     'L2_gnn_b2': (0.0, 0.276)}
    factors = {}
    for name, (base, spread) in spreads.items():
        noise = np.random.default_rng([zlib.crc32(name.encode()), seed]).standard_normal(out[name].shape)
        drawn = base * np.exp(spread * noise) if base else spread * noise
        out[name] = jnp.asarray(drawn.astype(out[name].dtype))
    for name, factor in factors.items():
        out[name] = (out[name] * factor).astype(out[name].dtype)
    return out
```

```python
import concourse.bass as bass
from concourse import mybir
from contextlib import ExitStack

P = 128
D = 96
N = 6250
E = 106250
ED0, ED2 = 17, 32
EPS = 1e-5

TILE = 128
TPC = 4
CHUNK = TILE * TPC
SLOTS = 4
CPH = 2
HALVES = SLOTS // CPH
HALF = CHUNK * CPH
STEP = CHUNK * SLOTS
ITERS = -(-E // STEP)
EP = ITERS * STEP

GT = 5
GROUP = GT * P
PAIRS = -(-N // (2 * GROUP))
GROUPS = 2 * PAIRS
NP = GROUPS * GROUP
NT = GROUPS * GT

BLK = 256
NBLK = EP // BLK
COLS = EP // P

FILTER, SUM, MAX = "filter", "sum", "max"
PASSES = [FILTER, SUM, SUM, MAX, MAX, SUM]

(M_W2_0, M_WS_0, M_WN_0, M_W1_1, M_W2_1, M_MSG1, M_ROOT1, M_MSG2, M_ROOT2, M_LIN, M_ROOT3) = range(11)
MATS = 11
(C_B1_0, C_B2_0, C_B_1, C_B_2, C_W_1, C_W_2, C_G_1, C_G_2, C_A_1, C_A_2) = range(10)
NCOL = 10
BF16_MAX = 3.3895313892515355e38


def at_least(engine, semaphore, value):
    if isinstance(value, int) and value <= 0:
        return
    engine.wait_ge(semaphore, value)


def settle(engine, tally):
    engine.sem_inc(tally, 1)


def build(nc, x, mats, cols, edge_w, eye, node_ids, src_idx, dst_shifted, blk_first, ea17, ea32, out):
    f32, bf16, i32 = mybir.dt.float32, mybir.dt.bfloat16, mybir.dt.int32
    ALU, ACT, AX = mybir.AluOpType, mybir.ActivationFunctionType, mybir.AxisListType

    with ExitStack() as ctx:
        def sb(name, shape, dt=f32):
            return ctx.enter_context(nc.sbuf_tensor(name, shape, dt))

        def sem(name):
            return ctx.enter_context(nc.semaphore(name))

        def dram(name, shape, dt=f32):
            return nc.dram_tensor(name, shape, dt, kind="Internal").ap()

        scan_rows = dram("scan_rows", (EP, D))
        keep_row = dram("keep_row", (1, EP), bf16)
        cap_row = dram("cap_row", (1, EP), bf16)
        dst_f = dram("dst_f", (EP, 1))
        cnt_row = dram("cnt_row", (1, NP + 1))
        x1 = dram("x1", (NP, D))
        h1 = dram("h1", (NP, D))
        x2 = dram("x2", (NP, D))
        t3 = dram("t3", (NP, D))
        c1 = dram("c1", (NP, D))
        t4 = dram("t4", (NP, D))
        x3 = dram("x3", (NP, D))
        t5 = dram("t5", (NP, D))
        tables = [x, x1, h1, t3, t4, t5]

        mats_sb = sb("mats_sb", [D + 1, MATS * D])
        cols_sb = sb("cols_sb", [D, NCOL])
        edge_w_sb = sb("edge_w_sb", [ED2, 3 * D])
        eye_sb = sb("eye_sb", [P, P])
        ids_sb = sb("ids_sb", [P, NT])
        eps_sb = sb("eps_sb", [P, 1])

        def mat(m):
            return mats_sb[:, m * D:(m + 1) * D]

        def col(c):
            return cols_sb[:, c:c + 1]

        dst_cur = sb("dst_cur", [P, COLS], i32)
        dst_prev = sb("dst_prev", [P, COLS], i32)
        dst_cur_f = sb("dst_cur_f", [P, COLS])
        keep_sb = sb("keep_sb", [P, COLS], bf16)
        cap_half = sb("cap_half", [P, COLS])
        cap_sb = sb("cap_sb", [P, COLS], bf16)
        first_i = sb("first_i", [P, NBLK], i32)
        first_f = sb("first_f", [P, NBLK])
        blk_le = sb("blk_le", [P, NBLK])
        blk_cnt = sb("blk_cnt", [P, NT])
        blk_f = sb("blk_f", [P, NT])
        blk_i = sb("blk_i", [P, NT], i32)
        blk_rows = [sb(f"blk_rows{h}", [P, BLK]) for h in range(2)]
        row_le = sb("row_le", [P, BLK])
        in_blk = sb("in_blk", [P, NT])
        cnt = sb("cnt", [P, NT])
        cnt_prev = sb("cnt_prev", [P, NT])
        zero_sb = sb("zero_sb", [1, 1])
        end_f = sb("end_f", [P, NT])
        end_i = sb("end_i", [P, NT], i32)
        deg = sb("deg", [P, NT])
        deg1 = sb("deg1", [P, NT])
        mask = sb("mask", [P, NT])
        dinv = sb("dinv", [P, NT])
        mask_dinv = sb("mask_dinv", [P, NT])

        idx = [sb(f"idx{h}", [P, CPH * TPC], i32) for h in range(HALVES)]
        flags = [sb(f"flags{h}", [D, HALF], bf16) for h in range(HALVES)]
        edge_in = [sb(f"edge_in{h}", [ED2, HALF]) for h in range(HALVES)]
        rows = [sb(f"rows{k}", [P, TPC * D]) for k in range(SLOTS)]
        hid = [sb(f"hid{k}", [D, CHUNK]) for k in range(2)]
        xt = [sb(f"xt{k}", [D, CHUNK]) for k in range(2)]
        msg = [sb(f"msg{k}", [D, CHUNK]) for k in range(2)]
        scan = [sb(f"scan{k}", [D, CHUNK]) for k in range(SLOTS)]
        back = [sb(f"back{k}", [P, TPC * D]) for k in range(SLOTS)]

        agg = [sb(f"agg{h}", [P, GT, D]) for h in range(2)]
        own = [sb(f"own{h}", [P, GT, D]) for h in range(2)]
        res = [sb(f"res{h}", [P, GT, D]) for h in range(2)]
        aggm = sb("aggm", [P, GT, D])
        own_t = sb("own_t", [D + 1, GROUP])
        agg_t = sb("agg_t", [D + 1, GROUP])
        new_t = sb("new_t", [D + 1, GROUP])
        z = sb("z", [P, GT, D])
        u = sb("u", [P, GT, D])
        y = sb("y", [P, GT, D])
        stats = sb("stats", [P, GT, 6])
        mv = sb("mv", [P, GT, 2])
        std = sb("std", [P, GT])
        rstd = sb("rstd", [P, GT])
        shift = sb("shift", [P, GT])
        new = [sb(f"new{h}", [P, GT, D]) for h in range(2)]
        tab = [sb(f"tab{h}", [P, GT, D]) for h in range(2)]
        conv = sb("conv", [D, NP])
        gn_out = sb("gn_out", [D, N])
        gn = sb("gn", [D, 8])

        bank = [ctx.enter_context(nc.psum_tensor(f"bank{b}", [P, 512], f32)) for b in range(8)]
        ps_x = [bank[0], bank[1]]
        ps_back = [bank[2], bank[3]]
        ps_hid = [bank[4], bank[5]]
        ps_w = [bank[6], bank[7]]
        ps_t = [bank[0], bank[1]]
        ps_t2 = [bank[2], bank[3]]
        ps_z = bank[4]
        ps_tab = bank[5]
        ps_c = [bank[6], bank[7]]
        TCUT = [(0, 4), (4, GT)]

        s_const = sem("s_const")
        s_eps = sem("s_eps")
        s_dst_in = sem("s_dst_in")
        s_dve = sem("s_dve")
        s_flag_out = sem("s_flag_out")
        s_blk_idx = sem("s_blk_idx")
        s_blk_in = [sem(f"s_blk_in{h}") for h in range(2)]
        s_blk_used = sem("s_blk_used")
        s_cnt = sem("s_cnt")
        s_cnt_out = sem("s_cnt_out")
        s_prev_in = sem("s_prev_in")
        s_deg1 = sem("s_deg1")
        s_sdeg = sem("s_sdeg")
        s_ends = sem("s_ends")
        s_flags_ready = sem("s_flags_ready")

        s_idx = [sem(f"s_idx{h}") for h in range(HALVES)]
        s_flags = [sem(f"s_flags{h}") for h in range(HALVES)]
        s_edge = [sem(f"s_edge{h}") for h in range(HALVES)]
        s_gath = [sem(f"s_gath{k}") for k in range(SLOTS)]
        s_xt = sem("s_xt")
        s_hid = sem("s_hid")
        s_relu = sem("s_relu")
        s_w = sem("s_w")
        s_xcopy = sem("s_xcopy")
        s_msg = sem("s_msg")
        s_scan = sem("s_scan")
        s_back = sem("s_back")
        s_evac = sem("s_evac")
        s_rows_out = [sem(f"s_rows_out{k}") for k in range(SLOTS)]

        s_tally_sp, s_tally_pool, s_tally_dve = (sem(f"s_tally_{e}") for e in ("sp", "pool", "dve"))

        block = ctx.enter_context(nc.Block())

        class Phase:

            def __init__(self, agg=True, own=None, res=None, wn=None, wroot=None, act=None, norm=False, out=None,
                         table=None, tmat=None, tscale=False, conv=None, finish=False, scale=None):
                self.agg, self.own, self.res, self.wn, self.wroot, self.act = agg, own, res, wn, wroot, act
                self.norm, self.out, self.table, self.tmat, self.tscale = norm, out, table, tmat, tscale
                self.conv, self.finish, self.scale = conv, finish, scale
                once, agg_t = GROUPS, wn is not None or conv is not None
                adds = {
                    "fetched": PAIRS * agg, "own": PAIRS * (own is not None), "res": PAIRS * (res is not None),
                    "new_out": PAIRS * (out is not None), "tab_out": PAIRS * (table is not None),
                    "masked": once * agg, "agg_tr": once * agg_t, "agg_ev": once * agg_t,
                    "own_tr": once * (wroot is not None), "own_ev": once * (wroot is not None),
                    "z": once * (conv is None), "pre": once * (conv is None and not finish and wn is None),
                    "u": once * (conv is None), "y": once * norm, "bn": once * norm, "mv": once * norm,
                    "std": once * norm, "rstd": once * norm, "prod": once * norm, "shift": once * norm,
                    "new": once * norm, "new_tr": once * (tmat is not None), "new_ev": once * (tmat is not None),
                    "tab": once * (tmat is not None), "tab_ev": once * (tmat is not None),
                    "conv": once * (conv is not None), "conv_ev": once * (conv is not None),
                    "gn": GN_STEPS * (conv is not None), "relu": once * finish,
                }
                self.start = dict(counts)
                self.made = "new" if norm else "u"
                for name, n in adds.items():
                    counts[name] = counts.get(name, 0) + n

            def after(self, name, n):
                return self.start.get(name, 0) + n

        counts = {}
        GN_STEPS = 7
        pair = {name: [sem(f"n_{name}{h}") for h in range(2)] for name in ("fetched", "own", "res", "new_out", "tab_out")}
        step = {name: sem("n_" + name) for name in (
            "masked", "agg_tr", "agg_ev", "own_tr", "own_ev", "z", "pre", "u", "y", "bn", "mv", "std", "rstd", "prod",
            "shift", "new", "new_tr", "new_ev", "tab", "tab_ev", "conv", "conv_ev", "gn", "relu")}

        n0 = Phase(own=x, wroot=M_WS_0, wn=M_WN_0, act="relu", norm=True, out=x1)
        n1 = Phase(conv=(M_W1_1, C_B_1, C_W_1, C_G_1, C_A_1))
        f1 = Phase(agg=False, own=x1, finish=True, out=h1)
        n2 = Phase(conv=(M_W2_1, C_B_2, C_W_2, C_G_2, C_A_2))
        f2 = Phase(agg=False, own=h1, res=x1, finish=True, norm=True, out=x2, table=t3, tmat=M_MSG1)
        n3 = Phase(own=x2, wroot=M_ROOT1, act="leaky", out=c1, table=t4, tmat=M_MSG2)
        n4 = Phase(own=c1, res=x2, wroot=M_ROOT2, act="leaky", norm=True, out=x3, table=t5, tmat=M_LIN, tscale=True)
        n5 = Phase(own=x3, wroot=M_ROOT3, act="relu", norm=True, out=out, scale=mask_dinv)
        PHASES = [[n0], [n1, f1], [n2, f2], [n3], [n4], [n5]]

        def group_rows(table, g):
            return table[bass.ds(g * GROUP, GROUP), :].rearrange("(p t) d -> p t d", p=P)

        @block.sync
        def _(sp):
            sp.dma_start(dst_cur[:], dst_shifted[1:EP + 1, :].rearrange("(p c) a -> p (c a)", p=P)).then_inc(s_dst_in, 16)
            sp.dma_start(dst_prev[:], dst_shifted[0:EP, :].rearrange("(p c) a -> p (c a)", p=P)).then_inc(s_dst_in, 16)
            sp.dma_start(first_i[:], blk_first.to_broadcast([P, NBLK])).then_inc(s_dst_in, 16)
            for dst_sb, src_dram in ((mats_sb, mats), (cols_sb, cols), (edge_w_sb, edge_w), (eye_sb, eye), (ids_sb, node_ids)):
                sp.dma_start(dst_sb[:], src_dram).then_inc(s_const, 16)
            sp.wait_ge(s_flags_ready, 1)
            sp.dma_start(dst_f.rearrange("(p c) a -> p (c a)", p=P), dst_cur_f[:]).then_inc(s_flag_out, 16)
            sp.dma_start(keep_row.rearrange("a (p c) -> (a p) c", p=P), keep_sb[:]).then_inc(s_flag_out, 16)
            sp.dma_start(cap_row.rearrange("a (p c) -> (a p) c", p=P), cap_sb[:]).then_inc(s_flag_out, 16)
            sp.wait_ge(s_cnt, 1)
            sp.dma_start(cnt_row[:, 0:1], zero_sb[:]).then_inc(s_cnt_out, 16)
            for g in range(GROUPS):
                sp.dma_start(cnt_row[0, 1 + g * GROUP:1 + (g + 1) * GROUP].rearrange("(p t) -> p t", p=P),
                             cnt[:, g * GT:(g + 1) * GT]).then_inc(s_cnt_out, 16)
            sp.wait_ge(s_cnt_out, 16 * (GROUPS + 1))
            for g in range(GROUPS):
                sp.dma_start(cnt_prev[:, g * GT:(g + 1) * GT],
                             cnt_row[0, g * GROUP:(g + 1) * GROUP].rearrange("(p t) -> p t", p=P)).then_inc(s_prev_in, 16)
            sp.wait_ge(s_flag_out, 48)

            for q, kind in enumerate(PASSES):
                flag_row = cap_row if kind == MAX else keep_row

                def load_idx(i, h):
                    sp.dma_start(idx[h][:], src_idx[bass.ds((i - q * ITERS) * HALVES + h, 1), :, :]
                                 .rearrange("a p c -> (a p) c")).then_inc(s_idx[h], 16)

                def load_edges(i, h):
                    e0 = ((i - q * ITERS) * HALVES + h) * HALF
                    sp.dma_start(flags[h][:], flag_row[:, bass.ds(e0, HALF)].to_broadcast([D, HALF])).then_inc(s_flags[h], 16)
                    if kind == FILTER:
                        sp.dma_start(edge_in[h][0:ED0, :], ea17[:, bass.ds(e0, HALF)]).then_inc(s_edge[h], 16)
                    if kind == MAX:
                        sp.dma_start(edge_in[h][:], ea32[:, bass.ds(e0, HALF)]).then_inc(s_edge[h], 16)

                def load_half(i, h):
                    for k in range(h * CPH, (h + 1) * CPH):
                        at_least(sp, s_gath[k], 16 * TPC * i)
                    settle(sp, s_tally_sp)
                    load_idx(i, h)
                    at_least(sp, s_scan, (i - 1) * SLOTS + (h + 1) * CPH)
                    settle(sp, s_tally_sp)
                    load_edges(i, h)

                for h in range(HALVES):
                    load_half(q * ITERS, h)
                with sp.Fori(q * ITERS + 1, (q + 1) * ITERS) as i:
                    for h in range(HALVES):
                        load_half(i, h)

                for ph in PHASES[q]:
                    if ph.conv:
                        continue

                    def load_group(g, h, half_n):
                        if ph.own is not None:
                            sp.dma_start(own[h][:], group_rows(ph.own, g)).then_inc(pair["own"][h], 16)
                        if ph.res is not None:
                            sp.dma_start(res[h][:], group_rows(ph.res, g)).then_inc(pair["res"][h], 16)

                    def store_group(g, h):
                        sp.wait_ge(step[ph.made], ph.after(ph.made, g + 1))
                        sp.dma_start(group_rows(ph.out, g), new[h][:]).then_inc(pair["new_out"][h], 16)
                        if ph.table is not None:
                            sp.wait_ge(step["tab_ev"], ph.after("tab_ev", g + 1))
                            sp.dma_start(group_rows(ph.table, g), tab[h][:]).then_inc(pair["tab_out"][h], 16)

                    for h in range(2):
                        load_group(h, h, 1)
                    with sp.Fori(0, PAIRS - 1) as j:
                        for h in range(2):
                            store_group(2 * j + h, h)
                            load_group(2 * j + 2 + h, h, j + 2)
                    for h in range(2):
                        store_group(GROUPS - 2 + h, h)
                    for h in range(2):
                        sp.wait_ge(pair["new_out"][h], 16 * ph.after("new_out", PAIRS))
                        if ph.table is not None:
                            sp.wait_ge(pair["tab_out"][h], 16 * ph.after("tab_out", PAIRS))

        @block.gpsimd
        def _(pool):
            pool.wait_ge(s_flag_out, 48)
            pool.wait_ge(s_blk_idx, 1)
            for t in range(NT):
                if t >= 2:
                    pool.wait_ge(s_blk_used, t - 1)
                pool.indirect_dma_start(blk_rows[t % 2][:], None, dst_f.rearrange("(b c) a -> b (c a)", c=BLK),
                                        bass.IndirectOffsetOnAxis(ap=blk_i[:, t:t + 1], axis=0)).then_inc(s_blk_in[t % 2], 16)

            for q, kind in enumerate(PASSES):
                def gather_chunk(i, k):
                    h = k // CPH
                    pool.wait_ge(s_idx[h], 16 * i + 16)
                    at_least(pool, s_xt, (i - 1) * SLOTS + k + 1)
                    settle(pool, s_tally_pool)
                    for j in range(TPC):
                        c = (k % CPH) * TPC + j
                        pool.indirect_dma_start(rows[k][:, j * D:(j + 1) * D], None, tables[q],
                                                bass.IndirectOffsetOnAxis(ap=idx[h][:, c:c + 1], axis=0)).then_inc(s_gath[k], 16)

                for k in range(SLOTS):
                    gather_chunk(q * ITERS, k)
                with pool.Fori(q * ITERS + 1, (q + 1) * ITERS) as i:
                    for k in range(SLOTS):
                        gather_chunk(i, k)

                ph = PHASES[q][0]
                for k in range(SLOTS):
                    pool.wait_ge(s_rows_out[k], 16 * (q + 1) * ITERS)
                if q == 0:
                    pool.wait_ge(s_ends, 1)
                for g in range(GROUPS):
                    if g >= 2:
                        pool.wait_ge(step["masked"], ph.after("masked", g - 1))
                    for t in range(GT):
                        pool.indirect_dma_start(agg[g % 2][:, t, :], None, scan_rows,
                                                bass.IndirectOffsetOnAxis(ap=end_i[:, g * GT + t:g * GT + t + 1], axis=0)
                                                ).then_inc(pair["fetched"][g % 2], 16)
                last = PHASES[q][-1]
                made = "tab_out" if last.table is not None else "new_out"
                for h in range(2):
                    pool.wait_ge(pair[made][h], 16 * last.after(made, PAIRS))

        @block.tensor
        def _(pe):
            pe.wait_ge(s_const, 80)
            for q, kind in enumerate(PASSES):
                def forward(i, k):
                    n, h, b = i * SLOTS + k, k // CPH, k % 2
                    lo = (k % CPH) * CHUNK
                    if kind == FILTER:
                        pe.wait_ge(s_edge[h], 16 * (i + 1))
                        at_least(pe, s_relu, n - 1)
                        nc.tensor.matmul(ps_hid[b][0:D, :], edge_w_sb[0:ED0, 0:D], edge_in[h][0:ED0, lo:lo + CHUNK],
                                         start=True, stop=True).then_inc(s_hid, 1)
                    pe.wait_ge(s_gath[k], 16 * TPC * (i + 1))
                    at_least(pe, s_scan, n - 1)
                    if kind == FILTER:
                        at_least(pe, s_xcopy, n - 1)
                    if kind == MAX:
                        pe.wait_ge(s_edge[h], 16 * (i + 1 - 2 * ITERS))
                        w = edge_w_sb[:, (q - 2) * D:(q - 1) * D]
                        nc.tensor.matmul(ps_x[b][0:D, :], w, edge_in[h][:, lo:lo + CHUNK], start=True, stop=False)
                        for j in range(TPC):
                            m = nc.tensor.matmul(ps_x[b][0:D, j::TPC], rows[k][:, j * D:(j + 1) * D], eye_sb[:],
                                                 start=False, stop=(j == TPC - 1))
                    else:
                        for j in range(TPC):
                            m = nc.tensor.transpose(ps_x[b][0:D, j::TPC], rows[k][:, j * D:(j + 1) * D], eye_sb[:])
                    m.then_inc(s_xt, 1)
                    if kind == FILTER:
                        pe.wait_ge(s_relu, n + 1)
                        at_least(pe, s_msg, n - 1)
                        nc.tensor.matmul(ps_w[b][0:D, :], mat(M_W2_0)[0:D, :], hid[b][:], start=True, stop=True).then_inc(s_w, 1)

                def backward(i, k):
                    n, b = i * SLOTS + k, k % 2
                    pe.wait_ge(s_scan, n + 1)
                    at_least(pe, s_evac, n - 1)
                    for j in range(TPC):
                        m = nc.tensor.transpose(ps_back[b][:, j * D:(j + 1) * D], scan[k][:, j::TPC], eye_sb[0:D, 0:D])
                    m.then_inc(s_back, 1)

                first = q * ITERS
                for k in range(SLOTS):
                    forward(first, k)
                    if k:
                        backward(first, k - 1)
                with pe.Fori(first + 1, first + ITERS) as i:
                    for k in range(SLOTS):
                        forward(i, k)
                        backward(i - 1 if k == 0 else i, (k - 1) % SLOTS)
                backward(first + ITERS - 1, SLOTS - 1)

                for ph in PHASES[q]:
                    def transpose_tiles(dst, src, semaphore):
                        for b, (a, e) in enumerate(TCUT):
                            for t in range(a, e):
                                m = nc.tensor.transpose(dst[b][0:D, (t - a) * P:(t - a + 1) * P], src[:, t, :], eye_sb[:])
                        m.then_inc(semaphore, 1)

                    def group(g, j, h):
                        if ph.conv:
                            pe.wait_ge(step["masked"], ph.after("masked", g + 1))
                            at_least(pe, step["agg_ev"], ph.after("agg_ev", g))
                            transpose_tiles(ps_t, aggm, step["agg_tr"])
                            pe.wait_ge(step["agg_ev"], ph.after("agg_ev", g + 1))
                            at_least(pe, step["conv_ev"], ph.after("conv_ev", g))
                            for c in range(2):
                                m = nc.tensor.matmul(ps_c[c][0:D, 0:GROUP // 2], mat(ph.conv[0])[0:D, :],
                                                     agg_t[0:D, c * GROUP // 2:(c + 1) * GROUP // 2], start=True, stop=True)
                            m.then_inc(step["conv"], 1)
                            return
                        if ph.finish:
                            pe.wait_ge(step["relu"], ph.after("relu", g + 1))
                            at_least(pe, step["u"], ph.after("u", g))
                            for t in range(GT):
                                m = nc.tensor.transpose(ps_z[:, t * D:(t + 1) * D], own_t[0:D, t::GT], eye_sb[0:D, 0:D])
                            m.then_inc(step["z"], 1)
                        else:
                            pe.wait_ge(pair["own"][h], 16 * ph.after("own", j + 1))
                            at_least(pe, step["own_ev"], ph.after("own_ev", g))
                            transpose_tiles(ps_t, own[h], step["own_tr"])
                            if ph.wn is not None:
                                pe.wait_ge(step["masked"], ph.after("masked", g + 1))
                                at_least(pe, step["agg_ev"], ph.after("agg_ev", g))
                                transpose_tiles(ps_t2, aggm, step["agg_tr"])
                                pe.wait_ge(step["agg_ev"], ph.after("agg_ev", g + 1))
                            pe.wait_ge(step["own_ev"], ph.after("own_ev", g + 1))
                            at_least(pe, step["u"], ph.after("u", g))
                            for t in range(GT):
                                m = nc.tensor.matmul(ps_z[:, t * D:(t + 1) * D], own_t[:, t * P:(t + 1) * P], mat(ph.wroot),
                                                     start=True, stop=ph.wn is None)
                                if ph.wn is not None:
                                    m = nc.tensor.matmul(ps_z[:, t * D:(t + 1) * D], agg_t[:, t * P:(t + 1) * P], mat(ph.wn),
                                                         start=False, stop=True)
                            m.then_inc(step["z"], 1)
                        if ph.tmat is not None:
                            pe.wait_ge(step[ph.made], ph.after(ph.made, g + 1))
                            at_least(pe, step["new_ev"], ph.after("new_ev", g))
                            transpose_tiles(ps_c, new[h], step["new_tr"])
                            pe.wait_ge(step["new_ev"], ph.after("new_ev", g + 1))
                            at_least(pe, step["tab_ev"], ph.after("tab_ev", g))
                            for t in range(GT):
                                m = nc.tensor.matmul(ps_tab[:, t * D:(t + 1) * D], new_t[:, t * P:(t + 1) * P], mat(ph.tmat),
                                                     start=True, stop=True)
                            m.then_inc(step["tab"], 1)

                    for h in range(2):
                        group(h, 0, h)
                    with pe.Fori(1, PAIRS) as j:
                        for h in range(2):
                            group(2 * j + h, j, h)

        @block.scalar
        def _(act):
            act.wait_ge(s_const, 80)
            act.wait_ge(s_eps, 1)
            act.wait_ge(s_deg1, 1)
            nc.scalar.activation(deg[:], deg1[:], ACT.Sqrt).then_inc(s_sdeg, 1)
            for q, kind in enumerate(PASSES):
                def forward(i, k):
                    n, b = i * SLOTS + k, k % 2
                    act.wait_ge(s_hid, n + 1)
                    at_least(act, s_w, n - 1)
                    nc.scalar.activation(hid[b][:], ps_hid[b][0:D, :], ACT.Relu, bias=col(C_B1_0)).then_inc(s_relu, 1)
                    act.wait_ge(s_xt, n + 1)
                    at_least(act, s_msg, n - 1)
                    nc.scalar.activation(xt[b][:], ps_x[b][0:D, :], ACT.Copy).then_inc(s_xcopy, 1)

                def backward(i, k):
                    n, b = i * SLOTS + k, k % 2
                    act.wait_ge(s_back, n + 1)
                    at_least(act, s_rows_out[k], 16 * i)
                    nc.scalar.activation(back[k][:], ps_back[b][:, 0:TPC * D], ACT.Copy).then_inc(s_evac, 1)
                    act.wait_ge(s_evac, n + 1)
                    e0 = (i - q * ITERS) * STEP + k * CHUNK
                    act.dma_start(scan_rows[bass.ds(e0, CHUNK), :].rearrange("(p j) d -> p (j d)", p=P), back[k][:]
                                  ).then_inc(s_rows_out[k], 16)

                first = q * ITERS
                for k in range(SLOTS):
                    if kind == FILTER:
                        forward(first, k)
                    if k:
                        backward(first, k - 1)
                with act.Fori(first + 1, first + ITERS) as i:
                    for k in range(SLOTS):
                        if kind == FILTER:
                            forward(i, k)
                        backward(i - 1 if k == 0 else i, (k - 1) % SLOTS)
                backward(first + ITERS - 1, SLOTS - 1)

                for ph in PHASES[q]:
                    def evacuate(dst, banks, semaphore):
                        for b, (a, e) in enumerate(TCUT):
                            m = nc.scalar.activation(dst[0:D, a * P:e * P], banks[b][0:D, 0:(e - a) * P], ACT.Copy)
                        m.then_inc(semaphore, 1)

                    def group(g, j, h):
                        if ph.conv:
                            act.wait_ge(step["agg_tr"], ph.after("agg_tr", g + 1))
                            at_least(act, step["conv"], ph.after("conv", g))
                            for b, (a, e) in enumerate(TCUT):
                                m = nc.scalar.activation(
                                    agg_t[0:D, :].rearrange("d (p t) -> d t p", t=GT)[:, a:e, :],
                                    ps_t[b][0:D, 0:(e - a) * P].rearrange("d (t p) -> d t p", p=P), ACT.Copy)
                            m.then_inc(step["agg_ev"], 1)
                            act.wait_ge(step["conv"], ph.after("conv", g + 1))
                            for c in range(2):
                                m = nc.scalar.activation(conv[:, bass.ds(g * GROUP + c * (GROUP // 2), GROUP // 2)],
                                                         ps_c[c][0:D, 0:GROUP // 2], ACT.Identity, bias=col(ph.conv[1]))
                            m.then_inc(step["conv_ev"], 1)
                            return
                        if ph.finish:
                            at_least(act, step["z"], ph.after("z", g))
                            nc.scalar.activation(own_t[0:D, :], conv[:, bass.ds(g * GROUP, GROUP)], ACT.Relu,
                                                 bias=gn[:, 7:8], scale=gn[:, 6:7]).then_inc(step["relu"], 1)
                        else:
                            act.wait_ge(step["own_tr"], ph.after("own_tr", g + 1))
                            at_least(act, step["z"], ph.after("z", g))
                            evacuate(own_t, ps_t, step["own_ev"])
                            if ph.wn is not None:
                                act.wait_ge(step["agg_tr"], ph.after("agg_tr", g + 1))
                                evacuate(agg_t, ps_t2, step["agg_ev"])
                        if ph.norm:
                            act.wait_ge(step["mv"], ph.after("mv", g + 1))
                            at_least(act, step["shift"], ph.after("shift", g))
                            nc.scalar.activation(std[:], mv[:, :, 1], ACT.Sqrt, bias=eps_sb[:]).then_inc(step["std"], 1)
                            act.wait_ge(step["shift"], ph.after("shift", g + 1))
                            at_least(act, pair["new_out"][h], 16 * ph.after("new_out", j))
                            if ph.tmat is not None:
                                at_least(act, step["new_tr"], ph.after("new_tr", g - 1))
                            for t in range(GT):
                                m = nc.scalar.activation(new[h][:, t, :], y[:, t, :], ACT.Identity,
                                                         bias=shift[:, t:t + 1], scale=rstd[:, t:t + 1])
                            m.then_inc(step["new"], 1)
                        if ph.tmat is not None:
                            act.wait_ge(step["new_tr"], ph.after("new_tr", g + 1))
                            at_least(act, step["tab"], ph.after("tab", g))
                            evacuate(new_t, ps_c, step["new_ev"])
                            act.wait_ge(step["tab"], ph.after("tab", g + 1))
                            at_least(act, pair["tab_out"][h], 16 * ph.after("tab_out", j))
                            if ph.tscale:
                                for t in range(GT):
                                    m = nc.scalar.activation(tab[h][:, t, :], ps_tab[:, t * D:(t + 1) * D], ACT.Copy,
                                                             scale=dinv[:, bass.ds(g * GT + t, 1)])
                            else:
                                m = nc.scalar.activation(tab[h][:].rearrange("p t d -> p (t d)"), ps_tab[:, 0:GT * D], ACT.Copy)
                            m.then_inc(step["tab_ev"], 1)

                    if ph.finish:
                        act.wait_ge(step["gn"], PHASES[q][0].after("gn", GN_STEPS))
                    for h in range(2):
                        group(h, 0, h)
                    with act.Fori(1, PAIRS) as j:
                        for h in range(2):
                            group(2 * j + h, j, h)
                    if ph.conv:
                        act.wait_ge(step["conv_ev"], ph.after("conv_ev", GROUPS))
                        nc.scalar.activation(gn_out[:], conv[:, 0:N], ACT.Identity, accum_out=gn[:, 0:1]).then_inc(step["gn"], 1)
                        act.wait_ge(step["gn"], ph.after("gn", 2))
                        nc.scalar.activation(gn_out[:], conv[:, 0:N], ACT.Square, bias=gn[:, 1:2], accum_out=gn[:, 2:3]).then_inc(step["gn"], 1)
                        act.wait_ge(step["gn"], ph.after("gn", 3))
                        nc.scalar.activation(gn[:, 3:4], gn[:, 2:3], ACT.Sqrt, scale=1.0 / N, bias=eps_sb[0:D, :]).then_inc(step["gn"], 1)

        @block.vector
        def _(dve):
            done = [0]

            def link(ins):
                done[0] += 1
                ins.then_inc(s_dve, 1)
                dve.wait_ge(s_dve, done[0])

            link(nc.vector.memset(zero_sb[:], 0.0))
            for t in (own_t, agg_t, new_t):
                link(nc.vector.memset(t[D:D + 1, :], 1.0))
            link(nc.vector.memset(scan[SLOTS - 1][:], 0.0))
            nc.vector.memset(eps_sb[:], EPS).then_inc(s_eps, 1)
            dve.wait_ge(s_dst_in, 48)
            nc.vector.tensor_copy(dst_cur_f[:], dst_cur[:])
            link(nc.vector.tensor_tensor(keep_sb[:], dst_cur[:], dst_prev[:], ALU.is_equal))
            link(nc.vector.tensor_scalar(cap_half[:], keep_sb[:], -0.5, BF16_MAX, ALU.add, ALU.mult))
            link(nc.vector.tensor_scalar(cap_sb[:], cap_half[:], 2.0, None, ALU.mult))
            link(nc.vector.tensor_copy(first_f[:], first_i[:]))
            dve.wait_ge(s_dve, done[0])
            nc.vector.tensor_copy(blk_f[0:1, 0:1], zero_sb[:]).then_inc(s_flags_ready, 1)
            dve.wait_ge(s_flags_ready, 1)
            dve.wait_ge(s_const, 80)
            base = done[0]
            with dve.Fori(0, NT) as t:
                nc.vector.tensor_scalar(blk_le[:], first_f[:], ids_sb[:, bass.ds(t, 1)], None, ALU.is_le, ALU.add,
                                        accum_out=blk_cnt[:, bass.ds(t, 1)]).then_inc(s_dve, 1)
                dve.wait_ge(s_dve, t + base + 1)
            done[0] += NT
            link(nc.vector.tensor_scalar(blk_f[:], blk_cnt[:], -1.0, 0.0, ALU.add, ALU.max))
            nc.vector.tensor_copy(blk_i[:], blk_f[:]).then_inc(s_blk_idx, 1)
            with dve.Fori(0, NT // 2) as j:
                for h in range(2):
                    t = 2 * j + h
                    dve.wait_ge(s_blk_in[h], 16 * j + 16)
                    nc.vector.tensor_scalar(row_le[:], blk_rows[h][:], ids_sb[:, bass.ds(t, 1)], None, ALU.is_le, ALU.add,
                                            accum_out=in_blk[:, bass.ds(t, 1)]).then_inc(s_blk_used, 1)
                    dve.wait_ge(s_blk_used, t + 1)
            nc.vector.scalar_tensor_tensor(out=cnt[:], in0=blk_f[:], scalar=float(BLK), in1=in_blk[:],
                                           op0=ALU.mult, op1=ALU.add).then_inc(s_cnt, 1)
            dve.wait_ge(s_cnt, 1)
            link(nc.vector.tensor_scalar(end_f[:], cnt[:], -1.0, 0.0, ALU.add, ALU.max))
            link(nc.vector.tensor_copy(end_i[:], end_f[:]))
            dve.wait_ge(s_prev_in, 16 * GROUPS)
            link(nc.vector.tensor_tensor(deg[:], cnt[:], cnt_prev[:], ALU.subtract))
            link(nc.vector.tensor_scalar(mask[:], deg[:], 1.0, None, ALU.min))
            nc.vector.tensor_scalar(deg1[:], deg[:], 1.0, None, ALU.max).then_inc(s_deg1, 1)
            dve.wait_ge(s_sdeg, 1)
            link(nc.vector.reciprocal(dinv[:], deg[:]))
            nc.vector.tensor_tensor(mask_dinv[:], mask[:], dinv[:], ALU.mult).then_inc(s_ends, 1)
            dve.wait_ge(s_ends, 1)

            for q, kind in enumerate(PASSES):
                op0, op1 = (ALU.min, ALU.max) if kind == MAX else (ALU.mult, ALU.add)

                def chunk(i, k):
                    n, h, b = i * SLOTS + k, k // CPH, k % 2
                    lo = (k % CPH) * CHUNK
                    dve.wait_ge(s_xt if kind != FILTER else s_w, n + 1)
                    data = ps_x[b][0:D, :]
                    if kind == FILTER:
                        dve.wait_ge(s_xcopy, n + 1)
                        at_least(dve, s_scan, n - 1)
                        nc.vector.scalar_tensor_tensor(out=msg[b][:], in0=ps_w[b][0:D, :], scalar=col(C_B2_0), in1=xt[b][:],
                                                       op0=ALU.add, op1=ALU.mult).then_inc(s_msg, 1)
                        dve.wait_ge(s_msg, n + 1)
                        data = msg[b][:]
                    dve.wait_ge(s_flags[h], 16 * (i + 1))
                    at_least(dve, s_back, n + 1 - SLOTS)
                    at_least(dve, s_scan, n)
                    nc.vector.tensor_tensor_scan(out=scan[k][:], data0=flags[h][:, lo:lo + CHUNK], data1=data,
                                                 initial=scan[(k - 1) % SLOTS][:, CHUNK - 1:CHUNK], op0=op0, op1=op1
                                                 ).then_inc(s_scan, 1)

                for k in range(SLOTS):
                    chunk(q * ITERS, k)
                with dve.Fori(q * ITERS + 1, (q + 1) * ITERS) as i:
                    for k in range(SLOTS):
                        chunk(i, k)

                for ph in PHASES[q]:
                    scale = mask if ph.scale is None else ph.scale

                    def group(g, j, h):
                        if ph.agg:
                            dve.wait_ge(pair["fetched"][h], 16 * GT * ph.after("fetched", j + 1))
                            if ph.wn is not None or ph.conv:
                                at_least(dve, step["agg_tr"], ph.after("agg_tr", g))
                            else:
                                at_least(dve, step["u"], ph.after("u", g))
                            nc.vector.tensor_tensor(
                                aggm[:], agg[h][:], scale[:, bass.ds(g * GT, GT)].unsqueeze(2).to_broadcast([P, GT, D]),
                                ALU.mult).then_inc(step["masked"], 1)
                        if ph.conv:
                            return
                        dve.wait_ge(step["z"], ph.after("z", g + 1))
                        z_ps = ps_z[:, 0:GT * D].rearrange("p (t d) -> p t d", t=GT)
                        target = new[h] if not ph.norm else u
                        if not ph.norm:
                            at_least(dve, pair["new_out"][h], 16 * ph.after("new_out", j))
                            if ph.tmat is not None:
                                at_least(dve, step["new_tr"], ph.after("new_tr", g - 1))
                        if ph.finish:
                            dve.wait_ge(pair["own"][h], 16 * ph.after("own", j + 1))
                            if ph.norm:
                                at_least(dve, step["y"], ph.after("y", g))
                            m = nc.vector.tensor_tensor(target[:], z_ps, own[h][:], ALU.add)
                            m.then_inc(step["u"], 1)
                            if not ph.norm:
                                return
                        elif ph.act == "relu" and ph.wn is not None:
                            at_least(dve, step["y"], ph.after("y", g))
                            nc.vector.tensor_scalar(u[:], z_ps, 0.0, None, ALU.max).then_inc(step["u"], 1)
                        else:
                            dve.wait_ge(step["masked"], ph.after("masked", g + 1))
                            nc.vector.tensor_tensor(z[:], z_ps, aggm[:], ALU.add).then_inc(step["pre"], 1)
                            dve.wait_ge(step["pre"], ph.after("pre", g + 1))
                            if ph.act == "relu":
                                nc.vector.tensor_scalar(target[:], z[:], 0.0, None, ALU.max).then_inc(step["u"], 1)
                            else:
                                nc.vector.scalar_tensor_tensor(out=target[:], in0=z[:], scalar=0.01, in1=z[:],
                                                               op0=ALU.mult, op1=ALU.max).then_inc(step["u"], 1)
                            if not ph.norm:
                                return
                        rest = own if ph.res is None else res
                        dve.wait_ge(step["u"], ph.after("u", g + 1))
                        rest_in = "own" if ph.res is None else "res"
                        dve.wait_ge(pair[rest_in][h], 16 * ph.after(rest_in, j + 1))
                        at_least(dve, step["new"], ph.after("new", g))
                        nc.vector.tensor_tensor(y[:], u[:], rest[h][:], ALU.add).then_inc(step["y"], 1)
                        dve.wait_ge(step["y"], ph.after("y", g + 1))
                        for t in range(GT):
                            m = nc.vector.bn_stats(stats[:, t, :], y[:, t, :])
                        m.then_inc(step["bn"], 1)
                        dve.wait_ge(step["bn"], ph.after("bn", g + 1))
                        at_least(dve, step["std"], ph.after("std", g))
                        settle(dve, s_tally_dve)
                        for t in range(GT):
                            m = nc.vector.bn_aggr(mv[:, t, :], stats[:, t, :])
                        m.then_inc(step["mv"], 1)
                        dve.wait_ge(step["std"], ph.after("std", g + 1))
                        nc.vector.reciprocal(rstd[:], std[:]).then_inc(step["rstd"], 1)
                        dve.wait_ge(step["rstd"], ph.after("rstd", g + 1))
                        dve.wait_ge(step["mv"], ph.after("mv", g + 1))
                        nc.vector.tensor_tensor(shift[:], mv[:, :, 0], rstd[:], ALU.mult).then_inc(step["prod"], 1)
                        dve.wait_ge(step["prod"], ph.after("prod", g + 1))
                        nc.vector.tensor_scalar(shift[:], shift[:], -1.0, None, ALU.mult).then_inc(step["shift"], 1)

                    for h in range(2):
                        group(h, 0, h)
                    with dve.Fori(1, PAIRS) as j:
                        for h in range(2):
                            group(2 * j + h, j, h)
                    if ph.conv:
                        _, _, w, bias, a = ph.conv
                        dve.wait_ge(step["gn"], ph.after("gn", 1))
                        nc.vector.tensor_scalar(gn[:, 1:2], gn[:, 0:1], col(a), -1.0 / N, ALU.mult, ALU.mult).then_inc(step["gn"], 1)
                        dve.wait_ge(step["gn"], ph.after("gn", 4))
                        nc.vector.reciprocal(gn[:, 4:5], gn[:, 3:4]).then_inc(step["gn"], 1)
                        dve.wait_ge(step["gn"], ph.after("gn", 5))
                        nc.vector.tensor_tensor(gn[:, 6:7], gn[:, 4:5], col(w), ALU.mult).then_inc(step["gn"], 1)
                        dve.wait_ge(step["gn"], ph.after("gn", 6))
                        nc.vector.tensor_scalar(gn[:, 7:8], gn[:, 1:2], gn[:, 6:7], col(bias), ALU.mult, ALU.add).then_inc(step["gn"], 1)


def kernel(**inputs):
    import numpy as np
    import concourse.bacc as bacc
    from concourse.bass_utils import run_bass_kernel_spmd

    v = {k: np.asarray(a) for k, a in inputs.items()}

    def rows_to(a, n):
        out = np.zeros((n,) + a.shape[1:], a.dtype)
        out[:a.shape[0]] = a
        return out

    def with_bias(w, b=None):
        out = np.zeros((D + 1, D), np.float32)
        out[:D] = w
        if b is not None:
            out[D] = b
        return out

    mats = np.concatenate([
        with_bias(v["L0_gnn_W2"].T), with_bias(v["L0_gnn_Ws"].T, v["L0_gnn_bs"]), with_bias(v["L0_gnn_Wn"].T, v["L0_gnn_bn"]),
        with_bias(v["L1_gnn_W1"]), with_bias(v["L1_gnn_W2"]),
        with_bias(v["L2_gnn_W1_msg"]), with_bias(v["L2_gnn_W1_root"], v["L2_gnn_b1"]),
        with_bias(v["L2_gnn_W2_msg"]), with_bias(v["L2_gnn_W2_root"], v["L2_gnn_b2"]),
        with_bias(v["L3_gnn_W_lin"].T, v["L3_gnn_b_lin"]), with_bias(v["L3_gnn_W_root"].T, v["L3_gnn_b_root"]),
    ], axis=1)
    cols = np.stack([v[n] for n in ("L0_gnn_b1", "L0_gnn_b2", "L1_gnn_b1", "L1_gnn_b2", "L1_gnn_gn1_w", "L1_gnn_gn2_w",
                                    "L1_gnn_gn1_b", "L1_gnn_gn2_b", "L1_gnn_gn1_a", "L1_gnn_gn2_a")], axis=1)
    edge_w = np.concatenate([rows_to(v["L0_gnn_W1"].T, ED2), v["L2_gnn_W1_edge"], v["L2_gnn_W2_edge"]], axis=1)
    src_idx = rows_to(v["src"], EP).reshape(EP // HALF, CPH, P, TPC).transpose(0, 2, 1, 3).reshape(EP // HALF, P, CPH * TPC)
    dst_shifted = np.full((EP + 1, 1), NP, np.int32)
    dst_shifted[1:E + 1, 0] = v["dst"]
    blk_first = dst_shifted[1::BLK, 0].reshape(1, NBLK)
    node_ids = np.arange(NP, dtype=np.float32).reshape(GROUPS, P, GT).transpose(1, 0, 2).reshape(P, NT)
    arrays = {
        "x": rows_to(v["x"], NP), "mats": mats, "cols": cols, "edge_w": edge_w, "eye": np.eye(P, dtype=np.float32),
        "node_ids": node_ids, "src_idx": src_idx, "dst_shifted": dst_shifted, "blk_first": blk_first,
        "ea17": rows_to(v["edge_attr_17"], EP).T, "ea32": rows_to(v["edge_attr_32"], EP).T,
    }
    arrays = {k: np.ascontiguousarray(a) for k, a in arrays.items()}
    nc = bacc.Bacc("TRN2", target_bir_lowering=False, num_devices=1)
    args = [nc.dram_tensor(k, a.shape, mybir.dt.from_np(a.dtype), kind="ExternalInput").ap() for k, a in arrays.items()]
    out = nc.dram_tensor("out", (NP, D), mybir.dt.float32, kind="ExternalOutput").ap()
    build(nc, *args, out)
    r = run_bass_kernel_spmd(nc, [arrays], core_ids=[0])
    return r.results[0]["out"][:N]
```

```python
import concourse.bass as bass
from concourse import mybir
from contextlib import ExitStack

P = 128
D = 96
N = 6250
E = 106250
ED0, ED2 = 17, 32
EPS = 1e-5

TILE = 128
TPC = 4
CHUNK = TILE * TPC
SLOTS = 8
BUFS = 4
ROUNDS = SLOTS // BUFS
CPH = 2
HALVES = SLOTS // CPH
HALF = CHUNK * CPH
STEP = CHUNK * SLOTS
ITERS = -(-E // STEP)
EP = ITERS * STEP

GT = 5
GROUP = GT * P
PAIRS = -(-N // (2 * GROUP))
GROUPS = 2 * PAIRS
NP = GROUPS * GROUP
NT = GROUPS * GT

BLK = 256
NBLK = EP // BLK
SEARCHES = ROUNDS * ITERS
assert SEARCHES >= NT
COLS = EP // P

PARTS = 3
STACK0 = 6 * ED0
STACK2 = PARTS * ED2
FLAT0 = ED0 * STEP // P
FLAT2 = ED2 * STEP // P
AHEAD = 2

FILTER, SUM, MAX = "filter", "sum", "max"
PASSES = [FILTER, SUM, SUM, MAX, MAX, SUM]

(M_W2_0, M_WS_0, M_WN_0, M_W1_1, M_W2_1, M_MSG1, M_ROOT1, M_MSG2, M_ROOT2, M_LIN, M_ROOT3) = range(11)
MATS = 11
(C_B1_0, C_B2_0, C_B_1, C_B_2, C_W_1, C_W_2, C_G_1, C_G_2, C_A_1, C_A_2) = range(10)
NCOL = 10
BF16_MAX = 3.3895313892515355e38


def at_least(engine, semaphore, value):
    if isinstance(value, int) and value <= 0:
        return
    engine.wait_ge(semaphore, value)


def settle(engine, tally):
    engine.sem_inc(tally, 1)


def before(i, k, lag):
    return i - (lag > k), (k - lag) % SLOTS


def within(g):
    return not isinstance(g, int) or 0 <= g < GROUPS


def over_groups(engine, step):
    for g in range(2):
        step(g, 0, g)
    with engine.Fori(1, PAIRS - 1) as j:
        for h in range(2):
            step(2 * j + h, j, h)
    for g in range(GROUPS - 2, GROUPS + 2):
        step(g, g // 2, g % 2)


def earlier(j, h, lag):
    return (j - 1 if lag > h else j) if lag < 2 else j - 1, (h - lag) % 2


def build(nc, x, mats, cols, edge_w, part_of, eye, node_ids, src_idx, dst_shifted, blk_first, ea17, ea32, out):
    f32, bf16, i32 = mybir.dt.float32, mybir.dt.bfloat16, mybir.dt.int32
    ALU, ACT, AX = mybir.AluOpType, mybir.ActivationFunctionType, mybir.AxisListType

    with ExitStack() as ctx:
        def sb(name, shape, dt=f32):
            return ctx.enter_context(nc.sbuf_tensor(name, shape, dt))

        def sem(name):
            return ctx.enter_context(nc.semaphore(name))

        def dram(name, shape, dt=f32):
            return nc.dram_tensor(name, shape, dt, kind="Internal").ap()

        parts0 = dram("parts0", (ITERS + AHEAD, PARTS, ED0, STEP), bf16)
        parts2 = dram("parts2", (ITERS, PARTS, ED2, STEP), bf16)
        scan_rows = dram("scan_rows", (EP, D))
        keep_row = dram("keep_row", (1, EP), bf16)
        cap_row = dram("cap_row", (1, EP), bf16)
        dst_f = dram("dst_f", (EP, 1))
        cnt_row = dram("cnt_row", (1, NP + 1))
        x1 = dram("x1", (NP, D))
        h1 = dram("h1", (NP, D))
        x2 = dram("x2", (NP, D))
        t3 = dram("t3", (NP, D))
        c1 = dram("c1", (NP, D))
        t4 = dram("t4", (NP, D))
        x3 = dram("x3", (NP, D))
        t5 = dram("t5", (NP, D))
        tables = [x, x1, h1, t3, t4, t5]

        mats_sb = sb("mats_sb", [D + 1, MATS * D])
        cols_sb = sb("cols_sb", [D, NCOL])
        edge_w_sb = sb("edge_w_sb", [STACK0, 3 * D])
        part_of_sb = sb("part_of_sb", [STACK0, PARTS])
        w_parts = sb("w_parts", [STACK0, PARTS, 3 * D], bf16)
        w_rest = sb("w_rest", [STACK0, 3 * D])
        w_stack = sb("w_stack", [STACK0, D], bf16)
        eye_sb = sb("eye_sb", [P, P])
        ids_sb = sb("ids_sb", [P, SEARCHES])
        eps_sb = sb("eps_sb", [P, 1])

        def mat(m):
            return mats_sb[:, m * D:(m + 1) * D]

        def col(c):
            return cols_sb[:, c:c + 1]

        dst_cur = sb("dst_cur", [P, COLS], i32)
        dst_prev = sb("dst_prev", [P, COLS], i32)
        dst_cur_f = sb("dst_cur_f", [P, COLS])
        keep_sb = sb("keep_sb", [P, COLS], bf16)
        cap_half = sb("cap_half", [P, COLS])
        cap_sb = sb("cap_sb", [P, COLS], bf16)
        first_i = sb("first_i", [P, NBLK], i32)
        first_f = sb("first_f", [P, NBLK])
        blk_le = sb("blk_le", [P, NBLK])
        blk_cnt = sb("blk_cnt", [P, 1])
        blk_f = sb("blk_f", [P, SEARCHES])
        blk_i = sb("blk_i", [P, 1], i32)
        blk_row = sb("blk_row", [P, BLK])
        row_le = sb("row_le", [P, BLK])
        in_blk = sb("in_blk", [P, SEARCHES])
        cnt = sb("cnt", [P, NT])
        cnt_prev = sb("cnt_prev", [P, NT])
        zero_sb = sb("zero_sb", [1, 1])
        end_f = sb("end_f", [P, NT])
        end_i = sb("end_i", [P, NT], i32)
        deg = sb("deg", [P, NT])
        deg1 = sb("deg1", [P, NT])
        deg_root = sb("deg_root", [P, NT])
        mask = sb("mask", [P, NT])
        dinv = sb("dinv", [P, NT])
        mask_dinv = sb("mask_dinv", [P, NT])

        idx = [sb(f"idx{h}", [P, CPH * TPC], i32) for h in range(HALVES)]
        flags = [sb(f"flags{h}", [D, HALF], bf16) for h in range(HALVES)]
        edge_in = [sb(f"edge_in{h}", [STACK0, HALF], bf16) for h in range(HALVES)]
        raw0 = [sb(f"raw0_{b}", [P, FLAT0]) for b in range(AHEAD)]
        rest0 = sb("rest0", [P, FLAT0])
        split0 = [sb(f"split0_{b}", [P, PARTS, FLAT0], bf16) for b in range(AHEAD)]
        raw2 = sb("raw2", [P, FLAT2])
        rest2 = sb("rest2", [P, FLAT2])
        split2 = sb("split2", [P, PARTS, FLAT2], bf16)
        rows = [sb(f"rows{k}", [P, TPC * D]) for k in range(SLOTS)]
        hid = [sb(f"hid{b}", [D + 1, CHUNK]) for b in range(2)]
        msg = [sb(f"msg{b}", [P, TPC * D]) for b in range(2)]
        scan = [sb(f"scan{k}", [D, CHUNK]) for k in range(BUFS)]
        back = [sb(f"back{k}", [P, TPC * D]) for k in range(BUFS)]

        agg = [sb(f"agg{h}", [P, GT, D]) for h in range(2)]
        own = [sb(f"own{h}", [P, GT, D]) for h in range(2)]
        res = [sb(f"res{h}", [P, GT, D]) for h in range(2)]
        aggm = [sb(f"aggm{h}", [P, GT, D]) for h in range(2)]
        own_t = [sb(f"own_t{h}", [D + 1, GROUP]) for h in range(2)]
        agg_t = [sb(f"agg_t{h}", [D + 1, GROUP]) for h in range(2)]
        new_t = sb("new_t", [D + 1, GROUP])
        z = sb("z", [P, GT, D])
        u = sb("u", [P, GT, D])
        y = [sb(f"y{h}", [P, GT, D]) for h in range(2)]
        stats = sb("stats", [P, GT, 6])
        mv = [sb(f"mv{h}", [P, GT, 2]) for h in range(2)]
        std = sb("std", [P, GT])
        rstd = sb("rstd", [P, GT])
        shift = sb("shift", [P, GT])
        new = [sb(f"new{h}", [P, GT, D]) for h in range(2)]
        tab = [sb(f"tab{h}", [P, GT, D]) for h in range(2)]
        conv = sb("conv", [D, NP])
        conv_stats = sb("conv_stats", [D, 2 * GROUPS, 6])
        gn_mv = sb("gn_mv", [D, 2])
        gn = sb("gn", [D, 8])
        (G_AMEAN, G_DIFF, G_VAR, G_STD, G_RSTD, G_SCALE, G_PROD, G_SHIFT) = range(8)

        def gcol(c):
            return gn[:, c:c + 1]

        bank = [ctx.enter_context(nc.psum_tensor(f"bank{b}", [P, 512], f32)) for b in range(8)]
        ps_x = [bank[0], bank[1]]
        ps_back = [bank[2], bank[3]]
        ps_hid = [bank[4], bank[5]]
        ps_w = [bank[6], bank[7]]
        ps_t = [bank[0], bank[1]]
        ps_t2 = [bank[2], bank[3]]
        ps_z = [bank[4], bank[5]]
        ps_tab = bank[6]
        ps_c = [bank[6], bank[7]]
        TCUT = [(0, 4), (4, GT)]

        s_const = sem("s_const")
        s_ones = sem("s_ones")
        s_dst_in = sem("s_dst_in")
        s_flag_made = sem("s_flag_made")
        s_flag_half = sem("s_flag_half")
        s_first_f = sem("s_first_f")
        s_flag_out = sem("s_flag_out")
        s_blk_cnt = sem("s_blk_cnt")
        s_blk_idx = sem("s_blk_idx")
        s_blk_in = sem("s_blk_in")
        s_in_blk = sem("s_in_blk")
        s_cnt = sem("s_cnt")
        s_end_f = sem("s_end_f")
        s_ends = sem("s_ends")
        s_cnt_out = sem("s_cnt_out")
        s_prev_in = sem("s_prev_in")
        s_deg = sem("s_deg")
        s_deg1 = sem("s_deg1")
        s_deg_root = sem("s_deg_root")
        s_dinv = sem("s_dinv")

        s_raw0, s_raw2 = sem("s_raw0"), sem("s_raw2")
        s_part0, s_part2 = sem("s_part0"), sem("s_part2")
        s_split0, s_split2 = sem("s_split0"), sem("s_split2")
        s_parts_out0, s_parts_out2 = sem("s_parts_out0"), sem("s_parts_out2")
        s_w_part = sem("s_w_part")
        s_w_stack = sem("s_w_stack")

        s_idx = [sem(f"s_idx{h}") for h in range(HALVES)]
        s_flags = [sem(f"s_flags{h}") for h in range(HALVES)]
        s_edge = [sem(f"s_edge{h}") for h in range(HALVES)]
        s_gath = [sem(f"s_gath{k}") for k in range(SLOTS)]
        s_hid = sem("s_hid")
        s_relu = sem("s_relu")
        s_w = sem("s_w")
        s_msg = sem("s_msg")
        s_xt = sem("s_xt")
        s_scan = sem("s_scan")
        s_back = sem("s_back")
        s_evac = sem("s_evac")
        s_rows_out = [sem(f"s_rows_out{k}") for k in range(BUFS)]
        s_tally_sp, s_tally_pool, s_tally_dve = (sem(f"s_tally_{e}") for e in ("sp", "pool", "dve"))

        GN_STEPS = 9
        pair = {name: [sem(f"n_{name}{h}") for h in range(2)] for name in ("fetched", "own", "res", "new_out", "tab_out")}
        step = {name: sem("n_" + name) for name in (
            "masked", "agg_tr", "agg_ev", "own_tr", "own_ev", "z", "pre", "u", "y", "bn", "mv", "std", "rstd",
            "shift", "new", "new_tr", "new_ev", "tab", "tab_ev", "conv", "conv_ev", "conv_bn", "gn", "relu")}
        counts = {}

        class NodePhase:

            def __init__(self, agg=True, own=None, res=None, wn=None, wroot=None, act=None, norm=False, out=None,
                         table=None, tmat=None, tscale=False, conv=None, finish=False, scale=None,
                         chain=(None,), made=None):
                self.agg, self.own, self.res, self.wn, self.wroot, self.act = agg, own, res, wn, wroot, act
                self.norm, self.out, self.table, self.tmat, self.tscale = norm, out, table, tmat, tscale
                self.conv, self.finish, self.scale = conv, finish, scale
                self.has_pre, self.has_u = "pre" in chain, "u" in chain
                self.opening, self.closing = chain[0], chain[-1]
                self.made = made
                every, by_agg = GROUPS, GROUPS * (wn is not None or conv is not None)
                by_table, by_root = GROUPS * (tmat is not None), GROUPS * (wroot is not None)
                adds = {
                    "fetched": PAIRS * agg, "own": PAIRS * (own is not None), "res": PAIRS * (res is not None),
                    "new_out": PAIRS * (out is not None), "tab_out": PAIRS * (table is not None),
                    "masked": every * agg, "agg_tr": by_agg, "agg_ev": by_agg, "own_tr": by_root, "own_ev": by_root,
                    "z": every * (conv is None), "pre": every * self.has_pre, "u": every * self.has_u,
                    "y": every * norm, "bn": every * norm, "mv": every * norm, "std": every * norm,
                    "rstd": every * norm, "shift": every * norm, "new": every * norm,
                    "new_tr": by_table, "new_ev": by_table, "tab": by_table, "tab_ev": by_table,
                    "conv": every * (conv is not None), "conv_ev": every * (conv is not None),
                    "conv_bn": every * (conv is not None), "gn": GN_STEPS * (conv is not None), "relu": every * finish,
                }
                self.start = {name: counts.get(name, 0) for name in adds}
                for name, n in adds.items():
                    counts[name] = self.start[name] + n

            def after(self, name, n):
                return self.start[name] + n

        n0 = NodePhase(own=x, wroot=M_WS_0, wn=M_WN_0, act="relu", norm=True, out=x1, chain=("y",), made="new")
        n1 = NodePhase(conv=(M_W1_1, C_B_1, C_W_1, C_G_1, C_A_1))
        f1 = NodePhase(agg=False, own=x1, finish=True, out=h1, chain=("u",), made="u")
        n2 = NodePhase(conv=(M_W2_1, C_B_2, C_W_2, C_G_2, C_A_2))
        f2 = NodePhase(agg=False, own=h1, res=x1, finish=True, norm=True, out=x2, table=t3, tmat=M_MSG1,
                       chain=("u", "y"), made="new")
        n3 = NodePhase(own=x2, wroot=M_ROOT1, act="leaky", out=c1, table=t4, tmat=M_MSG2, chain=("pre", "u"), made="u")
        n4 = NodePhase(own=c1, res=x2, wroot=M_ROOT2, act="leaky", norm=True, out=x3, table=t5, tmat=M_LIN, tscale=True,
                       chain=("pre", "u", "y"), made="new")
        n5 = NodePhase(own=x3, wroot=M_ROOT3, act="relu", norm=True, out=out, scale=mask_dinv,
                       chain=("pre", "y"), made="new")
        PHASES = [[n0], [n1, f1], [n2, f2], [n3], [n4], [n5]]

        def group_rows(table, g):
            return table[bass.ds(g * GROUP, GROUP), :].rearrange("(p t) d -> p t d", p=P)

        block = ctx.enter_context(nc.Block())

        @block.sync
        def _(sp):
            def edge_pass(q, kind):
                flag_row = cap_row if kind == MAX else keep_row

                def load_idx(i, h):
                    sp.dma_start(idx[h][:], src_idx[bass.ds((i - q * ITERS) * HALVES + h, 1), :, :]
                                 .rearrange("a p c -> (a p) c")).then_inc(s_idx[h], 16)

                def load_edges(i, h):
                    if kind == FILTER:
                        at = 0
                        for n in (PARTS, 2, 1):
                            sp.dma_start(edge_in[h][at:at + n * ED0, :],
                                         parts0[bass.ds(i, 1), 0:n, :, h * HALF:(h + 1) * HALF]
                                         .rearrange("a n f e -> (a n f) e")).then_inc(s_edge[h], 16)
                            at += n * ED0
                    if kind == MAX:
                        sp.dma_start(edge_in[h][0:STACK2, :],
                                     parts2[bass.ds(i - q * ITERS, 1), :, :, h * HALF:(h + 1) * HALF]
                                     .rearrange("a n f e -> (a n f) e")).then_inc(s_edge[h], 16)

                def load_raw0(i, b):
                    sp.dma_start(raw0[b][:], ea17[bass.ds(i, 1), :].rearrange("a (p c) -> (a p) c", p=P)).then_inc(s_raw0, 16)

                def store_parts0(i, b):
                    sp.wait_ge(s_split0, i + 1)
                    settle(sp, s_tally_sp)
                    sp.dma_start(parts0[bass.ds(i, 1)].rearrange("a n f e -> (a n f e)").rearrange("(n p c) -> p n c", n=PARTS, p=P),
                                 split0[b][:]).then_inc(s_parts_out0, 16)

                def load_raw2(i):
                    sp.dma_start(raw2[:], ea32[bass.ds(i, 1), :].rearrange("a (p c) -> (a p) c", p=P)).then_inc(s_raw2, 16)

                def store_parts2(i):
                    sp.wait_ge(s_split2, i + 1)
                    settle(sp, s_tally_sp)
                    sp.dma_start(parts2[bass.ds(i, 1)].rearrange("a n f e -> (a n f e)").rearrange("(n p c) -> p n c", n=PARTS, p=P),
                                 split2[:]).then_inc(s_parts_out2, 16)

                def load_flags(i, h):
                    e0 = ((i - q * ITERS) * HALVES + h) * HALF
                    sp.dma_start(flags[h][:], flag_row[:, bass.ds(e0, HALF)].to_broadcast([D, HALF])).then_inc(s_flags[h], 16)

                def load_half(i, h):
                    for k in range(h * CPH, (h + 1) * CPH):
                        at_least(sp, s_gath[k], 16 * TPC * i)
                    settle(sp, s_tally_sp)
                    load_idx(i, h)
                    at_least(sp, s_scan, (i - 1) * SLOTS + (h + 1) * CPH)
                    settle(sp, s_tally_sp)
                    load_edges(i, h)
                    load_flags(i, h)

                if q == 0:
                    for h in range(HALVES):
                        load_idx(0, h)
                    for b in range(AHEAD):
                        load_raw0(b, b)
                    sp.dma_start(dst_cur[:], dst_shifted[1:EP + 1, :].rearrange("(p c) a -> p (c a)", p=P)).then_inc(s_dst_in, 16)
                    sp.dma_start(dst_prev[:], dst_shifted[0:EP, :].rearrange("(p c) a -> p (c a)", p=P)).then_inc(s_dst_in, 16)
                    sp.dma_start(first_i[:], blk_first.to_broadcast([P, NBLK])).then_inc(s_dst_in, 16)
                    for dst_sb, src_dram in ((mats_sb, mats), (cols_sb, cols), (edge_w_sb, edge_w), (part_of_sb, part_of), (eye_sb, eye), (ids_sb, node_ids)):
                        sp.dma_start(dst_sb[:], src_dram).then_inc(s_const, 16)
                    for b in range(AHEAD):
                        store_parts0(b, b)
                    load_raw0(AHEAD, 0)
                    sp.wait_ge(s_parts_out0, 16 * AHEAD)
                    for h in range(HALVES):
                        load_edges(0, h)
                    sp.wait_ge(s_flag_made, 1)
                    sp.dma_start(keep_row.rearrange("a (p c) -> (a p) c", p=P), keep_sb[:]).then_inc(s_flag_out, 16)
                    sp.wait_ge(s_flag_made, 2)
                    sp.dma_start(dst_f.rearrange("(p c) a -> p (c a)", p=P), dst_cur_f[:]).then_inc(s_flag_out, 16)
                    sp.wait_ge(s_flag_made, 3)
                    sp.dma_start(cap_row.rearrange("a (p c) -> (a p) c", p=P), cap_sb[:]).then_inc(s_flag_out, 16)
                    sp.wait_ge(s_flag_out, 48)
                    for h in range(HALVES):
                        load_flags(0, h)
                else:
                    for h in range(HALVES):
                        load_half(q * ITERS, h)
                    if q == 1:
                        load_raw2(0)
                with sp.Fori(q * ITERS + 1, (q + 1) * ITERS) as i:
                    if q == 0:
                        sp.wait_ge(s_parts_out0, 16 * i + 16)
                        settle(sp, s_tally_sp)
                    for h in range(HALVES):
                        load_half(i, h)
                    if q == 0:
                        store_parts0(i + 1, 0)
                        load_raw0(i + AHEAD, 0)
                    if q == 1:
                        store_parts2(i - 1 - q * ITERS)
                        load_raw2(i - q * ITERS)
                if q == 1:
                    store_parts2(ITERS - 1)
                    sp.wait_ge(s_parts_out2, 16 * ITERS)

            def counts_shifted():
                sp.dma_start(cnt_row[:, 0:1], zero_sb[:]).then_inc(s_cnt_out, 16)
                sp.wait_ge(s_cnt, 1)
                sp.dma_start(cnt_row[0, 1:1 + NP].rearrange("(g p t) -> p g t", p=P, t=GT),
                             cnt[:].rearrange("p (g t) -> p g t", t=GT)).then_inc(s_cnt_out, 16)
                sp.wait_ge(s_cnt_out, 32)
                sp.dma_start(cnt_prev[:].rearrange("p (g t) -> p g t", t=GT),
                             cnt_row[0, 0:NP].rearrange("(g p t) -> p g t", p=P, t=GT)).then_inc(s_prev_in, 16)

            def node_phase(ph):
                def load_group(g, h):
                    if ph.own is not None:
                        sp.dma_start(own[h][:], group_rows(ph.own, g)).then_inc(pair["own"][h], 16)
                    if ph.res is not None:
                        sp.dma_start(res[h][:], group_rows(ph.res, g)).then_inc(pair["res"][h], 16)

                def one(g, j, h):
                    if within(g) and within(g + 2):
                        at_least(sp, step[ph.closing], ph.after(ph.closing, g + 1))
                        load_group(g + 2, h)
                    if within(g - 1):
                        _, b = earlier(j, h, 1)
                        sp.wait_ge(step[ph.made], ph.after(ph.made, g))
                        sp.dma_start(group_rows(ph.out, g - 1), new[b][:]).then_inc(pair["new_out"][b], 16)
                    if ph.table is not None and within(g - 2):
                        sp.wait_ge(step["tab_ev"], ph.after("tab_ev", g - 1))
                        sp.dma_start(group_rows(ph.table, g - 2), tab[h][:]).then_inc(pair["tab_out"][h], 16)

                for h in range(2):
                    load_group(h, h)
                over_groups(sp, one)
                for h in range(2):
                    sp.wait_ge(pair["new_out"][h], 16 * ph.after("new_out", PAIRS))
                    if ph.table is not None:
                        sp.wait_ge(pair["tab_out"][h], 16 * ph.after("tab_out", PAIRS))

            for q, kind in enumerate(PASSES):
                edge_pass(q, kind)
                if q == 0:
                    counts_shifted()
                for ph in PHASES[q]:
                    if ph.conv is None:
                        node_phase(ph)

        @block.gpsimd
        def _(pool):
            def edge_pass(q, kind):
                def gather_chunk(i, k):
                    h = k // CPH
                    pool.wait_ge(s_idx[h], 16 * i + 16)
                    at_least(pool, s_xt, (i - 1) * SLOTS + k + 1)
                    settle(pool, s_tally_pool)
                    for j in range(TPC):
                        c = (k % CPH) * TPC + j
                        pool.indirect_dma_start(rows[k][:, j * D:(j + 1) * D], None, tables[q],
                                                bass.IndirectOffsetOnAxis(ap=idx[h][:, c:c + 1], axis=0)).then_inc(s_gath[k], 16)

                def gather_block(t):
                    pool.wait_ge(s_blk_idx, t + 1)
                    at_least(pool, s_in_blk, t)
                    settle(pool, s_tally_pool)
                    pool.indirect_dma_start(blk_row[:], None, dst_f.rearrange("(b c) a -> b (c a)", c=BLK),
                                            bass.IndirectOffsetOnAxis(ap=blk_i[:], axis=0)).then_inc(s_blk_in, 16)

                def iteration(i):
                    for k in range(SLOTS):
                        gather_chunk(i, k)
                        if q == 0 and k % BUFS == BUFS - 1:
                            if isinstance(i, int):
                                pool.wait_ge(s_flag_out, 48)
                            gather_block(i * ROUNDS + k // BUFS)

                iteration(q * ITERS)
                with pool.Fori(q * ITERS + 1, (q + 1) * ITERS) as i:
                    iteration(i)

            def fetch(q, ph):
                for k in range(BUFS):
                    pool.wait_ge(s_rows_out[k], 16 * (q + 1) * ITERS * ROUNDS)
                if q == 0:
                    pool.wait_ge(s_ends, 1)
                for g in range(GROUPS):
                    at_least(pool, step["masked"], ph.after("masked", g - 1) if g >= 2 else 0)
                    for t in range(GT):
                        pool.indirect_dma_start(agg[g % 2][:, t, :], None, scan_rows,
                                                bass.IndirectOffsetOnAxis(ap=end_i[:, g * GT + t:g * GT + t + 1], axis=0)
                                                ).then_inc(pair["fetched"][g % 2], 16)

            for q, kind in enumerate(PASSES):
                edge_pass(q, kind)
                fetch(q, PHASES[q][0])
                last = PHASES[q][-1]
                table = "tab_out" if last.table is not None else "new_out"
                for h in range(2):
                    pool.wait_ge(pair[table][h], 16 * last.after(table, PAIRS))

        @block.tensor
        def _(pe):
            def edge_pass(q, kind):
                def hidden(i, k):
                    n, h, b = i * SLOTS + k, k // CPH, k % 2
                    lo = (k % CPH) * CHUNK
                    pe.wait_ge(s_edge[h], 16 * PARTS * (i + 1))
                    at_least(pe, s_relu, n - 1)
                    nc.tensor.matmul(ps_hid[b][0:D, :], w_stack[:], edge_in[h][:, lo:lo + CHUNK],
                                     start=True, stop=True).then_inc(s_hid, 1)

                def filters(i, k):
                    n, b = i * SLOTS + k, k % 2
                    pe.wait_ge(s_relu, n + 1)
                    at_least(pe, s_msg, n - 1)
                    for j in range(TPC):
                        m = nc.tensor.matmul(ps_w[b][:, j * D:(j + 1) * D], hid[b][:, j::TPC], mat(M_W2_0), start=True, stop=True)
                    m.then_inc(s_w, 1)

                def forward(i, k):
                    n, h, b = i * SLOTS + k, k // CPH, k % 2
                    lo = (k % CPH) * CHUNK
                    if kind == FILTER:
                        pe.wait_ge(s_msg, n + 1)
                    else:
                        pe.wait_ge(s_gath[k], 16 * TPC * (i + 1))
                    at_least(pe, s_scan, n - 1)
                    source = msg[b] if kind == FILTER else rows[k]
                    if kind == MAX:
                        pe.wait_ge(s_edge[h], 16 * (i + 1))
                        for part in range(PARTS):
                            n_rows = (PARTS - part) * ED2
                            nc.tensor.matmul(ps_x[b][0:D, :], w_parts[0:n_rows, part, (q - 2) * D:(q - 1) * D],
                                             edge_in[h][0:n_rows, lo:lo + CHUNK], start=(part == 0), stop=False)
                        for j in range(TPC):
                            m = nc.tensor.matmul(ps_x[b][0:D, j::TPC], source[:, j * D:(j + 1) * D], eye_sb[:],
                                                 start=False, stop=(j == TPC - 1))
                    else:
                        for j in range(TPC):
                            m = nc.tensor.transpose(ps_x[b][0:D, j::TPC], source[:, j * D:(j + 1) * D], eye_sb[:])
                    m.then_inc(s_xt, 1)

                def backward(i, k):
                    n, b = i * SLOTS + k, k % 2
                    pe.wait_ge(s_scan, n + 1)
                    at_least(pe, s_evac, n - 1)
                    for j in range(TPC):
                        m = nc.tensor.transpose(ps_back[b][:, j * D:(j + 1) * D], scan[k % BUFS][:, j::TPC], eye_sb[0:D, 0:D])
                    m.then_inc(s_back, 1)

                def chunk(i, k, behind):
                    if kind == FILTER:
                        hidden(i, k)
                        if behind >= 1:
                            forward(*before(i, k, 1))
                        filters(i, k)
                        if behind >= 2:
                            backward(*before(i, k, 2))
                    else:
                        forward(i, k)
                        if behind >= 1:
                            backward(*before(i, k, 1))

                first, last = q * ITERS, (q + 1) * ITERS - 1
                for k in range(SLOTS):
                    chunk(first, k, k)
                with pe.Fori(first + 1, last + 1) as i:
                    for k in range(SLOTS):
                        chunk(i, k, SLOTS)
                if kind == FILTER:
                    forward(last, SLOTS - 1)
                    backward(last, SLOTS - 2)
                backward(last, SLOTS - 1)

            def transpose_tiles(dst, src, semaphore):
                for b, (a, e) in enumerate(TCUT):
                    for t in range(a, e):
                        m = nc.tensor.transpose(dst[b][0:D, (t - a) * P:(t - a + 1) * P], src[:, t, :], eye_sb[:])
                m.then_inc(semaphore, 1)

            def conv_phase(ph):
                def one(g, j, h):
                    if within(g):
                        pe.wait_ge(step["masked"], ph.after("masked", g + 1))
                        at_least(pe, step["agg_ev"], ph.after("agg_ev", g))
                        transpose_tiles(ps_t, aggm[h], step["agg_tr"])
                    if within(g - 1):
                        _, b = earlier(j, h, 1)
                        pe.wait_ge(step["agg_ev"], ph.after("agg_ev", g))
                        at_least(pe, step["conv_ev"], ph.after("conv_ev", g - 1))
                        for c in range(2):
                            m = nc.tensor.matmul(ps_c[c][0:D, 0:GROUP // 2], mat(ph.conv[0])[0:D, :],
                                                 agg_t[b][0:D, c * GROUP // 2:(c + 1) * GROUP // 2], start=True, stop=True)
                        m.then_inc(step["conv"], 1)
                over_groups(pe, one)

            def node_phase(ph):
                def one(g, j, h):
                    if within(g) and not ph.finish:
                        pe.wait_ge(pair["own"][h], 16 * ph.after("own", j + 1))
                        at_least(pe, step["own_ev"], ph.after("own_ev", g))
                        transpose_tiles(ps_t, own[h], step["own_tr"])
                        if ph.wn is not None:
                            pe.wait_ge(step["masked"], ph.after("masked", g + 1))
                            at_least(pe, step["agg_ev"], ph.after("agg_ev", g))
                            transpose_tiles(ps_t2, aggm[h], step["agg_tr"])
                    if ph.tmat is not None and within(g - 2):
                        pe.wait_ge(step[ph.made], ph.after(ph.made, g - 1))
                        at_least(pe, step["new_ev"], ph.after("new_ev", g - 2))
                        transpose_tiles(ps_t2, new[h], step["new_tr"])
                    if within(g):
                        at_least(pe, step[ph.opening], ph.after(ph.opening, g - 1))
                        if ph.finish:
                            pe.wait_ge(step["relu"], ph.after("relu", g + 1))
                            for t in range(GT):
                                m = nc.tensor.transpose(ps_z[h][:, t * D:(t + 1) * D], own_t[h][0:D, t::GT], eye_sb[0:D, 0:D])
                        else:
                            pe.wait_ge(step["own_ev"], ph.after("own_ev", g + 1))
                            if ph.wn is not None:
                                pe.wait_ge(step["agg_ev"], ph.after("agg_ev", g + 1))
                            for t in range(GT):
                                m = nc.tensor.matmul(ps_z[h][:, t * D:(t + 1) * D], own_t[h][:, t * P:(t + 1) * P], mat(ph.wroot),
                                                     start=True, stop=ph.wn is None)
                                if ph.wn is not None:
                                    m = nc.tensor.matmul(ps_z[h][:, t * D:(t + 1) * D], agg_t[h][:, t * P:(t + 1) * P], mat(ph.wn),
                                                         start=False, stop=True)
                        m.then_inc(step["z"], 1)
                    if ph.tmat is not None and within(g - 2):
                        pe.wait_ge(step["new_ev"], ph.after("new_ev", g - 1))
                        at_least(pe, step["tab_ev"], ph.after("tab_ev", g - 2))
                        for t in range(GT):
                            m = nc.tensor.matmul(ps_tab[:, t * D:(t + 1) * D], new_t[:, t * P:(t + 1) * P], mat(ph.tmat),
                                                 start=True, stop=True)
                        m.then_inc(step["tab"], 1)
                over_groups(pe, one)

            pe.wait_ge(s_const, 96)
            pe.wait_ge(s_ones, 1)
            pe.wait_ge(s_w_stack, PARTS)
            for q, kind in enumerate(PASSES):
                edge_pass(q, kind)
                for ph in PHASES[q]:
                    if ph.conv is not None:
                        conv_phase(ph)
                    else:
                        node_phase(ph)

        @block.scalar
        def _(act):
            def edge_pass(q, kind):
                def hidden(i, k):
                    n, b = i * SLOTS + k, k % 2
                    act.wait_ge(s_hid, n + 1)
                    at_least(act, s_w, n - 1)
                    nc.scalar.activation(hid[b][0:D, :], ps_hid[b][0:D, :], ACT.Relu, bias=col(C_B1_0)).then_inc(s_relu, 1)

                def backward(i, k):
                    n, b, m = i * SLOTS + k, k % 2, k % BUFS
                    act.wait_ge(s_back, n + 1)
                    at_least(act, s_rows_out[m], 16 * (i * ROUNDS + k // BUFS))
                    nc.scalar.activation(back[m][:], ps_back[b][:, 0:TPC * D], ACT.Copy).then_inc(s_evac, 1)
                    act.wait_ge(s_evac, n + 1)
                    e0 = (i - q * ITERS) * STEP + k * CHUNK
                    act.dma_start(scan_rows[bass.ds(e0, CHUNK), :].rearrange("(p j) d -> p (j d)", p=P), back[m][:]
                                  ).then_inc(s_rows_out[m], 16)

                lag = 2 if kind == FILTER else 1

                def chunk(i, k, behind):
                    if kind == FILTER:
                        hidden(i, k)
                    if behind >= lag:
                        backward(*before(i, k, lag))

                first, last = q * ITERS, (q + 1) * ITERS - 1
                for k in range(SLOTS):
                    chunk(first, k, k)
                with act.Fori(first + 1, last + 1) as i:
                    for k in range(SLOTS):
                        chunk(i, k, SLOTS)
                for k in range(SLOTS - lag, SLOTS):
                    backward(last, k)

            def evacuate(dst, banks, semaphore):
                for b, (a, e) in enumerate(TCUT):
                    m = nc.scalar.activation(dst[0:D, a * P:e * P], banks[b][0:D, 0:(e - a) * P], ACT.Copy)
                m.then_inc(semaphore, 1)

            def conv_phase(ph):
                def one(g, j, h):
                    if within(g):
                        act.wait_ge(step["agg_tr"], ph.after("agg_tr", g + 1))
                        at_least(act, step["conv"], ph.after("conv", g - 1))
                        for b, (a, e) in enumerate(TCUT):
                            m = nc.scalar.activation(agg_t[h][0:D, :].rearrange("d (p t) -> d t p", t=GT)[:, a:e, :],
                                                     ps_t[b][0:D, 0:(e - a) * P].rearrange("d (t p) -> d t p", p=P), ACT.Copy)
                        m.then_inc(step["agg_ev"], 1)
                    if within(g - 1):
                        act.wait_ge(step["conv"], ph.after("conv", g))
                        for c in range(2):
                            m = nc.scalar.activation(conv[:, bass.ds((g - 1) * GROUP + c * (GROUP // 2), GROUP // 2)],
                                                     ps_c[c][0:D, 0:GROUP // 2], ACT.Identity, bias=col(ph.conv[1]))
                        m.then_inc(step["conv_ev"], 1)
                over_groups(act, one)
                act.wait_ge(step["gn"], ph.after("gn", 4))
                nc.scalar.activation(gcol(G_STD), gcol(G_VAR), ACT.Sqrt, bias=eps_sb[0:D, :]).then_inc(step["gn"], 1)
                act.wait_ge(step["gn"], ph.after("gn", GN_STEPS))

            def node_phase(ph):
                def one(g, j, h):
                    if within(g):
                        at_least(act, step["z"], ph.after("z", g - 1))
                        if ph.finish:
                            nc.scalar.activation(own_t[h][0:D, :], conv[:, bass.ds(g * GROUP, GROUP)], ACT.Relu,
                                                 bias=gcol(G_SHIFT), scale=gcol(G_SCALE)).then_inc(step["relu"], 1)
                        else:
                            act.wait_ge(step["own_tr"], ph.after("own_tr", g + 1))
                            evacuate(own_t[h], ps_t, step["own_ev"])
                            if ph.wn is not None:
                                act.wait_ge(step["agg_tr"], ph.after("agg_tr", g + 1))
                                evacuate(agg_t[h], ps_t2, step["agg_ev"])
                    if ph.tmat is not None and within(g - 2):
                        act.wait_ge(step["new_tr"], ph.after("new_tr", g - 1))
                        at_least(act, step["tab"], ph.after("tab", g - 2))
                        evacuate(new_t, ps_t2, step["new_ev"])
                    if ph.norm and within(g - 1):
                        i, b = earlier(j, h, 1)
                        act.wait_ge(step["mv"], ph.after("mv", g))
                        at_least(act, step["rstd"], ph.after("rstd", g - 1))
                        nc.scalar.activation(std[:], mv[b][:, :, 1], ACT.Sqrt, bias=eps_sb[:]).then_inc(step["std"], 1)
                        act.wait_ge(step["shift"], ph.after("shift", g))
                        at_least(act, pair["new_out"][b], 16 * ph.after("new_out", i))
                        if ph.tmat is not None:
                            at_least(act, step["new_tr"], ph.after("new_tr", g - 2))
                        for t in range(GT):
                            m = nc.scalar.activation(new[b][:, t, :], y[b][:, t, :], ACT.Identity,
                                                     bias=shift[:, t:t + 1], scale=rstd[:, t:t + 1])
                        m.then_inc(step["new"], 1)
                    if ph.tmat is not None and within(g - 2):
                        act.wait_ge(step["tab"], ph.after("tab", g - 1))
                        at_least(act, pair["tab_out"][h], 16 * ph.after("tab_out", j - 1))
                        if ph.tscale:
                            for t in range(GT):
                                m = nc.scalar.activation(tab[h][:, t, :], ps_tab[:, t * D:(t + 1) * D], ACT.Copy,
                                                         scale=dinv[:, bass.ds((g - 2) * GT + t, 1)])
                        else:
                            m = nc.scalar.activation(tab[h][:].rearrange("p t d -> p (t d)"), ps_tab[:, 0:GT * D], ACT.Copy)
                        m.then_inc(step["tab_ev"], 1)
                over_groups(act, one)

            act.wait_ge(s_const, 96)
            for q, kind in enumerate(PASSES):
                edge_pass(q, kind)
                if q == 0:
                    act.wait_ge(s_deg1, 1)
                    nc.scalar.activation(deg_root[:], deg1[:], ACT.Sqrt).then_inc(s_deg_root, 1)
                for ph in PHASES[q]:
                    if ph.conv is not None:
                        conv_phase(ph)
                    else:
                        node_phase(ph)

        @block.vector
        def _(dve):
            def make_flags():
                dve.wait_ge(s_dst_in, 48)
                nc.vector.tensor_tensor(keep_sb[:], dst_cur[:], dst_prev[:], ALU.is_equal).then_inc(s_flag_made, 1)
                nc.vector.tensor_copy(dst_cur_f[:], dst_cur[:]).then_inc(s_flag_made, 1)
                dve.wait_ge(s_flag_made, 2)
                nc.vector.tensor_scalar(cap_half[:], keep_sb[:], -0.5, BF16_MAX, ALU.add, ALU.mult).then_inc(s_flag_half, 1)
                dve.wait_ge(s_flag_half, 1)
                nc.vector.tensor_scalar(cap_sb[:], cap_half[:], 2.0, None, ALU.mult).then_inc(s_flag_made, 1)
                nc.vector.memset(zero_sb[:], 0.0)
                nc.vector.memset(scan[BUFS - 1][:], 0.0)
                nc.vector.memset(eps_sb[:], EPS)
                for t in (*own_t, *agg_t, new_t, *hid):
                    m = nc.vector.memset(t[D:D + 1, :], 1.0)
                m.then_inc(s_ones, 1)
                nc.vector.tensor_copy(first_f[:], first_i[:]).then_inc(s_first_f, 1)
                dve.wait_ge(s_first_f, 1)
                dve.wait_ge(s_ones, 1)
                dve.wait_ge(s_const, 96)

            def split_weights():
                def part(ins):
                    part.done += 1
                    ins.then_inc(s_w_part, 1)
                    dve.wait_ge(s_w_part, part.done)

                part.done = 0
                part(nc.vector.tensor_copy(w_parts[:, 0, :], edge_w_sb[:]))
                part(nc.vector.tensor_tensor(w_rest[:], edge_w_sb[:], w_parts[:, 0, :], ALU.subtract))
                part(nc.vector.tensor_copy(w_parts[:, 1, :], w_rest[:]))
                part(nc.vector.tensor_tensor(w_parts[:, 2, :], w_rest[:], w_parts[:, 1, :], ALU.subtract))
                nc.vector.tensor_scalar(w_stack[:], w_parts[:, 0, 0:D], part_of_sb[:, 0:1], None, ALU.mult).then_inc(s_w_stack, 1)
                for n in range(1, PARTS):
                    dve.wait_ge(s_w_stack, n)
                    nc.vector.scalar_tensor_tensor(out=w_stack[:], in0=w_parts[:, n, 0:D], scalar=part_of_sb[:, n:n + 1],
                                                   in1=w_stack[:], op0=ALU.mult, op1=ALU.add).then_inc(s_w_stack, 1)

            def split(raw, rest, parts, i, steps, made):
                nc.vector.tensor_copy(parts[:, 0, :], raw[:]).then_inc(steps, 1)
                dve.wait_ge(steps, 3 * i + 1)
                nc.vector.tensor_tensor(rest[:], raw[:], parts[:, 0, :], ALU.subtract).then_inc(steps, 1)
                dve.wait_ge(steps, 3 * i + 2)
                nc.vector.tensor_scalar(parts[:, 1, :], rest[:], 1.0, None, ALU.mult).then_inc(steps, 1)
                dve.wait_ge(steps, 3 * i + 3)
                nc.vector.tensor_tensor(parts[:, 2, :], rest[:], parts[:, 1, :], ALU.subtract).then_inc(made, 1)
                dve.wait_ge(made, i + 1)

            def split_layer0(i, b):
                dve.wait_ge(s_raw0, 16 * max(i + 1, AHEAD) if isinstance(i, int) else 16 * (i + 1))
                if not isinstance(i, int) or i >= AHEAD:
                    dve.wait_ge(s_parts_out0, 16 * i)
                split(raw0[b], rest0, split0[b], i, s_part0, s_split0)

            def split_layer2(i):
                dve.wait_ge(s_raw2, 16 * i + 16)
                at_least(dve, s_parts_out2, 16 * i)
                split(raw2, rest2, split2, i, s_part2, s_split2)

            def count_in_block(i):
                dve.wait_ge(s_blk_in, 16 * i + 16)
                nc.vector.tensor_scalar(row_le[:], blk_row[:], ids_sb[:, bass.ds(i, 1)], None, ALU.is_le, ALU.add,
                                        accum_out=in_blk[:, bass.ds(i, 1)]).then_inc(s_in_blk, 1)
                dve.wait_ge(s_in_blk, i + 1)

            def find_block(i):
                nc.vector.tensor_scalar(blk_le[:], first_f[:], ids_sb[:, bass.ds(i, 1)], None, ALU.is_le, ALU.add,
                                        accum_out=blk_cnt[:]).then_inc(s_blk_cnt, 1)
                dve.wait_ge(s_blk_cnt, i + 1)
                nc.vector.tensor_scalar(blk_f[:, bass.ds(i, 1)], blk_cnt[:], -1.0, 0.0, ALU.add, ALU.max)
                nc.vector.tensor_scalar(blk_i[:], blk_cnt[:], -1.0, 0.0, ALU.add, ALU.max).then_inc(s_blk_idx, 1)
                dve.wait_ge(s_blk_idx, i + 1)

            def make_ends():
                nc.vector.scalar_tensor_tensor(out=cnt[:], in0=blk_f[:, 0:NT], scalar=float(BLK), in1=in_blk[:, 0:NT],
                                               op0=ALU.mult, op1=ALU.add).then_inc(s_cnt, 1)
                dve.wait_ge(s_cnt, 1)
                nc.vector.tensor_scalar(end_f[:], cnt[:], -1.0, 0.0, ALU.add, ALU.max).then_inc(s_end_f, 1)
                dve.wait_ge(s_end_f, 1)
                nc.vector.tensor_copy(end_i[:], end_f[:]).then_inc(s_ends, 1)
                dve.wait_ge(s_prev_in, 16)
                nc.vector.tensor_tensor(deg[:], cnt[:], cnt_prev[:], ALU.subtract).then_inc(s_deg, 1)
                dve.wait_ge(s_deg, 1)
                nc.vector.tensor_scalar(deg1[:], deg[:], 1.0, None, ALU.max).then_inc(s_deg1, 1)
                nc.vector.tensor_scalar(mask[:], deg[:], 1.0, None, ALU.min)
                dve.wait_ge(s_deg_root, 1)
                nc.vector.reciprocal(dinv[:], deg_root[:]).then_inc(s_dinv, 1)
                dve.wait_ge(s_dinv, 1)
                nc.vector.tensor_tensor(mask_dinv[:], mask[:], dinv[:], ALU.mult).then_inc(s_dinv, 1)
                dve.wait_ge(s_dinv, 2)

            def edge_pass(q, kind):
                op0, op1 = (ALU.min, ALU.max) if kind == MAX else (ALU.mult, ALU.add)

                def filtered(i, k):
                    n, b = i * SLOTS + k, k % 2
                    dve.wait_ge(s_w, n + 1)
                    dve.wait_ge(s_gath[k], 16 * TPC * (i + 1))
                    at_least(dve, s_xt, n - 1)
                    nc.vector.tensor_tensor(msg[b][:], ps_w[b][:, 0:TPC * D], rows[k][:], ALU.mult).then_inc(s_msg, 1)

                def reduce(i, k):
                    n, h, b = i * SLOTS + k, k // CPH, k % 2
                    lo = (k % CPH) * CHUNK
                    dve.wait_ge(s_xt, n + 1)
                    dve.wait_ge(s_flags[h], 16 * (i + 1))
                    at_least(dve, s_back, n + 1 - BUFS)
                    at_least(dve, s_scan, n)
                    nc.vector.tensor_tensor_scan(out=scan[k % BUFS][:], data0=flags[h][:, lo:lo + CHUNK], data1=ps_x[b][0:D, :],
                                                 initial=scan[(k - 1) % BUFS][:, CHUNK - 1:CHUNK], op0=op0, op1=op1
                                                 ).then_inc(s_scan, 1)

                def chunk(i, k, behind):
                    if kind == FILTER:
                        filtered(i, k)
                        if behind >= 1:
                            reduce(*before(i, k, 1))
                    else:
                        reduce(i, k)

                first, last = q * ITERS, (q + 1) * ITERS - 1

                def iteration(i, behind):
                    if q == 1:
                        split_layer2(i - q * ITERS)
                    for k in range(SLOTS):
                        if q == 0 and k % BUFS == 0:
                            t = i * ROUNDS + k // BUFS
                            if not isinstance(t, int) or t > 0:
                                count_in_block(t - 1)
                            find_block(t)
                        chunk(i, k, behind + k)
                    if q == 0:
                        split_layer0(i + AHEAD, 0)

                iteration(first, 0)
                with dve.Fori(first + 1, last + 1) as i:
                    iteration(i, SLOTS)
                if kind == FILTER:
                    reduce(last, SLOTS - 1)

            def masked(ph, g, j, h):
                scale = mask if ph.scale is None else ph.scale
                dve.wait_ge(pair["fetched"][h], 16 * GT * ph.after("fetched", j + 1))
                if ph.has_pre:
                    at_least(dve, step["pre"], ph.after("pre", g - 1))
                else:
                    at_least(dve, step["agg_tr"], ph.after("agg_tr", g - 1))
                nc.vector.tensor_tensor(aggm[h][:], agg[h][:],
                                        scale[:, bass.ds(g * GT, GT)].unsqueeze(2).to_broadcast([P, GT, D]),
                                        ALU.mult).then_inc(step["masked"], 1)

            def conv_phase(ph):
                def one(g, j, h):
                    if within(g):
                        masked(ph, g, j, h)
                    if within(g - 2):
                        dve.wait_ge(step["conv_ev"], ph.after("conv_ev", g - 1))
                        for c in range(2):
                            n0 = (g - 2) * GROUP + c * (GROUP // 2)
                            width = min(GROUP // 2, N - n0) if isinstance(g, int) else GROUP // 2
                            m = nc.vector.bn_stats(conv_stats[:, bass.ds(2 * (g - 2) + c, 1), :].rearrange("d a s -> d (a s)"),
                                                   conv[:, bass.ds(n0, width)])
                        m.then_inc(step["conv_bn"], 1)
                over_groups(dve, one)
                _, _, w, bias, a = ph.conv
                gn_step = iter(range(1, GN_STEPS + 1))

                def gn_after(instruction):
                    instruction.then_inc(step["gn"], 1)
                    dve.wait_ge(step["gn"], ph.after("gn", next(gn_step)))

                dve.wait_ge(step["conv_bn"], ph.after("conv_bn", GROUPS))
                gn_after(nc.vector.bn_aggr(gn_mv[:], conv_stats[:].rearrange("d a s -> d (a s)")))
                gn_after(nc.vector.tensor_tensor(gcol(G_AMEAN), gn_mv[:, 0:1], col(a), ALU.mult))
                gn_after(nc.vector.tensor_tensor(gcol(G_DIFF), gn_mv[:, 0:1], gcol(G_AMEAN), ALU.subtract))
                gn_after(nc.vector.scalar_tensor_tensor(out=gcol(G_VAR), in0=gcol(G_DIFF), scalar=gcol(G_DIFF),
                                                        in1=gn_mv[:, 1:2], op0=ALU.mult, op1=ALU.add))
                dve.wait_ge(step["gn"], ph.after("gn", next(gn_step)))
                gn_after(nc.vector.reciprocal(gcol(G_RSTD), gcol(G_STD)))
                gn_after(nc.vector.tensor_tensor(gcol(G_SCALE), gcol(G_RSTD), col(w), ALU.mult))
                gn_after(nc.vector.tensor_tensor(gcol(G_PROD), gcol(G_AMEAN), gcol(G_SCALE), ALU.mult))
                gn_after(nc.vector.tensor_tensor(gcol(G_SHIFT), col(bias), gcol(G_PROD), ALU.subtract))

            def node_phase(ph):
                def one(g, j, h):
                    if within(g) and ph.agg:
                        masked(ph, g, j, h)
                    if ph.norm and within(g - 1):
                        _, b = earlier(j, h, 1)
                        dve.wait_ge(step["std"], ph.after("std", g))
                        at_least(dve, step["new"], ph.after("new", g - 1))
                        nc.vector.reciprocal(rstd[:], std[:]).then_inc(step["rstd"], 1)
                        dve.wait_ge(step["rstd"], ph.after("rstd", g))
                        nc.vector.scalar_tensor_tensor(out=shift[:], in0=mv[b][:, :, 0], scalar=-1.0, in1=rstd[:],
                                                       op0=ALU.mult, op1=ALU.mult).then_inc(step["shift"], 1)
                    if not within(g):
                        return
                    dve.wait_ge(step["z"], ph.after("z", g + 1))
                    now = ps_z[h][:, 0:GT * D].rearrange("p (t d) -> p t d", t=GT)
                    if ph.has_pre:
                        at_least(dve, step[ph.closing], ph.after(ph.closing, g))
                        dve.wait_ge(step["masked"], ph.after("masked", g + 1))
                        nc.vector.tensor_tensor(z[:], now, aggm[h][:], ALU.add).then_inc(step["pre"], 1)
                        dve.wait_ge(step["pre"], ph.after("pre", g + 1))
                        now = z[:]
                    if ph.has_u:
                        if ph.norm:
                            at_least(dve, step["y"], ph.after("y", g))
                        else:
                            at_least(dve, pair["new_out"][h], 16 * ph.after("new_out", j))
                            if ph.tmat is not None:
                                at_least(dve, step["new_tr"], ph.after("new_tr", g - 1))
                        target = u if ph.norm else new[h]
                        if ph.finish:
                            dve.wait_ge(pair["own"][h], 16 * ph.after("own", j + 1))
                            nc.vector.tensor_tensor(target[:], now, own[h][:], ALU.add).then_inc(step["u"], 1)
                        else:
                            nc.vector.scalar_tensor_tensor(out=target[:], in0=now, scalar=0.01, in1=now,
                                                           op0=ALU.mult, op1=ALU.max).then_inc(step["u"], 1)
                        dve.wait_ge(step["u"], ph.after("u", g + 1))
                        now = u[:]
                    if not ph.norm:
                        return
                    rest, rest_in = (own, "own") if ph.res is None else (res, "res")
                    dve.wait_ge(pair[rest_in][h], 16 * ph.after(rest_in, j + 1))
                    at_least(dve, step["new"], ph.after("new", g - 1))
                    if ph.act == "relu":
                        m = nc.vector.scalar_tensor_tensor(out=y[h][:], in0=now, scalar=0.0, in1=rest[h][:],
                                                           op0=ALU.max, op1=ALU.add)
                    else:
                        m = nc.vector.tensor_tensor(y[h][:], now, rest[h][:], ALU.add)
                    m.then_inc(step["y"], 1)
                    dve.wait_ge(step["y"], ph.after("y", g + 1))
                    at_least(dve, step["mv"], ph.after("mv", g))
                    for t in range(GT):
                        m = nc.vector.bn_stats(stats[:, t, :], y[h][:, t, :])
                    m.then_inc(step["bn"], 1)
                    at_least(dve, step["std"], ph.after("std", g - 1))
                    dve.wait_ge(step["bn"], ph.after("bn", g + 1))
                    settle(dve, s_tally_dve)
                    for t in range(GT):
                        m = nc.vector.bn_aggr(mv[h][:, t, :], stats[:, t, :])
                    m.then_inc(step["mv"], 1)
                over_groups(dve, one)

            for b in range(AHEAD):
                split_layer0(b, b)
            make_flags()
            split_weights()
            for q, kind in enumerate(PASSES):
                edge_pass(q, kind)
                if q == 0:
                    count_in_block(SEARCHES - 1)
                    make_ends()
                for ph in PHASES[q]:
                    if ph.conv is not None:
                        conv_phase(ph)
                    else:
                        node_phase(ph)


def kernel(**inputs):
    import numpy as np
    import concourse.bacc as bacc
    from concourse.bass_utils import run_bass_kernel_spmd

    v = {k: np.asarray(a) for k, a in inputs.items()}

    def rows_to(a, n):
        out = np.zeros((n,) + a.shape[1:], a.dtype)
        out[:a.shape[0]] = a
        return out

    def with_bias(w, b=None):
        out = np.zeros((D + 1, D), np.float32)
        out[:D] = w
        if b is not None:
            out[D] = b
        return out

    mats = np.concatenate([
        with_bias(v["L0_gnn_W2"].T, v["L0_gnn_b2"]), with_bias(v["L0_gnn_Ws"].T, v["L0_gnn_bs"]), with_bias(v["L0_gnn_Wn"].T, v["L0_gnn_bn"]),
        with_bias(v["L1_gnn_W1"]), with_bias(v["L1_gnn_W2"]),
        with_bias(v["L2_gnn_W1_msg"]), with_bias(v["L2_gnn_W1_root"], v["L2_gnn_b1"]),
        with_bias(v["L2_gnn_W2_msg"]), with_bias(v["L2_gnn_W2_root"], v["L2_gnn_b2"]),
        with_bias(v["L3_gnn_W_lin"].T, v["L3_gnn_b_lin"]), with_bias(v["L3_gnn_W_root"].T, v["L3_gnn_b_root"]),
    ], axis=1)
    cols = np.stack([v[n] for n in ("L0_gnn_b1", "L0_gnn_b2", "L1_gnn_b1", "L1_gnn_b2", "L1_gnn_gn1_w", "L1_gnn_gn2_w",
                                    "L1_gnn_gn1_b", "L1_gnn_gn2_b", "L1_gnn_gn1_a", "L1_gnn_gn2_a")], axis=1)
    edge_w = np.concatenate([np.tile(v["L0_gnn_W1"].T, (6, 1))] + [
        rows_to(np.tile(v[n], (PARTS, 1)), STACK0) for n in ("L2_gnn_W1_edge", "L2_gnn_W2_edge")], axis=1)
    part_of = np.repeat(np.eye(PARTS, dtype=np.float32), (3 * ED0, 2 * ED0, ED0), axis=0)

    def by_iteration(a, iterations):
        out = np.zeros((iterations, a.shape[1] * STEP), a.dtype)
        out[:ITERS] = rows_to(a, EP).reshape(ITERS, STEP, -1).transpose(0, 2, 1).reshape(ITERS, -1)
        return out

    src_idx = rows_to(v["src"], EP).reshape(EP // HALF, CPH, P, TPC).transpose(0, 2, 1, 3).reshape(EP // HALF, P, CPH * TPC)
    dst_shifted = np.full((EP + 1, 1), NP, np.int32)
    dst_shifted[1:E + 1, 0] = v["dst"]
    blk_first = dst_shifted[1::BLK, 0].reshape(1, NBLK)
    node_ids = np.zeros((P, SEARCHES), np.float32)
    node_ids[:, :NT] = np.arange(NP, dtype=np.float32).reshape(GROUPS, P, GT).transpose(1, 0, 2).reshape(P, NT)
    arrays = {
        "x": rows_to(v["x"], NP), "mats": mats, "cols": cols, "edge_w": edge_w, "part_of": part_of, "eye": np.eye(P, dtype=np.float32),
        "node_ids": node_ids, "src_idx": src_idx, "dst_shifted": dst_shifted, "blk_first": blk_first,
        "ea17": by_iteration(v["edge_attr_17"], ITERS + AHEAD), "ea32": by_iteration(v["edge_attr_32"], ITERS),
    }
    arrays = {k: np.ascontiguousarray(a) for k, a in arrays.items()}
    nc = bacc.Bacc("TRN2", target_bir_lowering=False, num_devices=1)
    args = [nc.dram_tensor(k, a.shape, mybir.dt.from_np(a.dtype), kind="ExternalInput").ap() for k, a in arrays.items()]
    out = nc.dram_tensor("out", (NP, D), mybir.dt.float32, kind="ExternalOutput").ap()
    build(nc, *args, out)
    r = run_bass_kernel_spmd(nc, [arrays], core_ids=[0])
    return r.results[0]["out"][:N]
```

```python
import concourse.bass as bass
from concourse import mybir
from contextlib import ExitStack

P = 128
D = 96
N = 6250
E = 106250
ED0, ED2 = 17, 32
EPS = 1e-5

TILE = 128
TPC = 4
CHUNK = TILE * TPC
SLOTS = 8
BUFS = 4
ROUNDS = SLOTS // BUFS
CPH = 2
HALVES = SLOTS // CPH
HALF = CHUNK * CPH
STEP = CHUNK * SLOTS
ITERS = -(-E // STEP)
EP = ITERS * STEP

GT = 5
GROUP = GT * P
PAIRS = -(-N // (2 * GROUP))
GROUPS = 2 * PAIRS
NP = GROUPS * GROUP
NT = GROUPS * GT

HIGHS = NP // P
NO_FRACTION = 1.5 * 2 ** 23
ROOT_SLOTS = 2
NT_ROOM = ROOT_SLOTS * ITERS
assert NT_ROOM >= NT and SLOTS == 4 * ROOT_SLOTS
COLS = EP // P

PARTS = 3
STACK0 = 6 * ED0
STACK2 = PARTS * ED2
FLAT0 = ED0 * STEP // P
FLAT2 = ED2 * STEP // P
AHEAD = 2

FILTER, SUM, MAX = "filter", "sum", "max"
PASSES = [FILTER, SUM, SUM, MAX, MAX, SUM]

(M_W2_0, M_WS_0, M_WN_0, M_W1_1, M_W2_1, M_MSG1, M_ROOT1, M_MSG2, M_ROOT2, M_LIN, M_ROOT3) = range(11)
MATS = 11
(C_B1_0, C_B2_0, C_B_1, C_B_2, C_W_1, C_W_2, C_G_1, C_G_2, C_A_1, C_A_2) = range(10)
NCOL = 10
BF16_MAX = 3.3895313892515355e38


def at_least(engine, semaphore, value):
    if isinstance(value, int) and value <= 0:
        return
    engine.wait_ge(semaphore, value)


def settle(engine, tally):
    engine.sem_inc(tally, 1)


def before(i, k, lag):
    return i - (lag > k), (k - lag) % SLOTS


def within(g):
    return not isinstance(g, int) or 0 <= g < GROUPS


def over_groups(engine, step):
    for g in range(2):
        step(g, 0, g)
    with engine.Fori(1, PAIRS - 1) as j:
        for h in range(2):
            step(2 * j + h, j, h)
    for g in range(GROUPS - 2, GROUPS + 2):
        step(g, g // 2, g % 2)


def earlier(j, h, lag):
    return (j - 1 if lag > h else j) if lag < 2 else j - 1, (h - lag) % 2


def build(nc, x, mats, cols, edge_w, part_of, eye, digits, lower, src_idx, dst_shifted, ea17, ea32, out):
    f32, bf16, i32 = mybir.dt.float32, mybir.dt.bfloat16, mybir.dt.int32
    ALU, ACT, AX = mybir.AluOpType, mybir.ActivationFunctionType, mybir.AxisListType

    with ExitStack() as ctx:
        def sb(name, shape, dt=f32):
            return ctx.enter_context(nc.sbuf_tensor(name, shape, dt))

        def sem(name):
            return ctx.enter_context(nc.semaphore(name))

        def dram(name, shape, dt=f32):
            return nc.dram_tensor(name, shape, dt, kind="Internal").ap()

        parts0 = dram("parts0", (ITERS + AHEAD, PARTS, ED0, STEP), bf16)
        parts2 = dram("parts2", (ITERS, PARTS, ED2, STEP), bf16)
        scan_rows = dram("scan_rows", (EP, D))
        keep_row = dram("keep_row", (1, EP), bf16)
        cap_row = dram("cap_row", (1, EP), bf16)
        cnt_row = dram("cnt_row", (1, NP + 1))
        x1 = dram("x1", (NP, D))
        h1 = dram("h1", (NP, D))
        x2 = dram("x2", (NP, D))
        t3 = dram("t3", (NP, D))
        c1 = dram("c1", (NP, D))
        t4 = dram("t4", (NP, D))
        x3 = dram("x3", (NP, D))
        t5 = dram("t5", (NP, D))
        tables = [x, x1, h1, t3, t4, t5]

        mats_sb = sb("mats_sb", [D + 1, MATS * D])
        cols_sb = sb("cols_sb", [D, NCOL])
        edge_w_sb = sb("edge_w_sb", [STACK0, 3 * D])
        part_of_sb = sb("part_of_sb", [STACK0, PARTS])
        w_parts = sb("w_parts", [STACK0, PARTS, 3 * D], bf16)
        w_rest = sb("w_rest", [STACK0, 3 * D])
        w_stack = sb("w_stack", [STACK0, D], bf16)
        averaging = sb("averaging", [D, D])
        w_centred = sb("w_centred", [D, D])
        eye_sb = sb("eye_sb", [P, P])
        lower_sb = sb("lower_sb", [HIGHS, HIGHS])
        eps_sb = sb("eps_sb", [P, 1])

        def mat(m):
            return mats_sb[:, m * D:(m + 1) * D]

        def col(c):
            return cols_sb[:, c:c + 1]

        rows_a = sb("rows_a", [P, NT_ROOM, D])
        room_b = sb("room_b", [P, NT_ROOM * D])
        rows_b = room_b[:].rearrange("p (n d) -> p n d", d=D)
        lo = [COLS, 2 * COLS] + [2 * COLS + (b + 1) * FLAT0 for b in range(AHEAD + 1)]
        dst_cur_f, cap_half = room_b[:, 0:lo[0]], room_b[:, lo[0]:lo[1]]
        raw0 = [room_b[:, lo[1 + b]:lo[2 + b]] for b in range(AHEAD)]
        rest0 = room_b[:, lo[1 + AHEAD]:lo[2 + AHEAD]]
        assert lo[2 + AHEAD] <= NT * D
        room_c = sb("room_c", [P, NP])
        root_all = room_c[:, 0:NT_ROOM * D].rearrange("p (n d) -> p n d", d=D)
        conv = room_c[0:D, :]
        raw2, rest2 = room_c[:, 0:FLAT2], room_c[:, FLAT2:2 * FLAT2]
        assert NT_ROOM * D <= NP
        root_in = sb("root_in", [P, D])
        root_t = sb("root_t", [D + 1, P])
        room_d = sb("room_d", [P, NT_ROOM * P])
        sum_t = room_d[0:D, :]
        low, high = room_d[:, 0:COLS], room_d[:, COLS:2 * COLS]
        lo = 2 * COLS + 2 * CHUNK
        digits_sb = room_d[:, lo:lo + TPC * (P + HIGHS)]
        all_lows = digits_sb[:, 0:TPC * P].rearrange("p (j l) -> p j l", j=TPC)
        all_highs = digits_sb[:, TPC * P:].rearrange("p (j h) -> p j h", j=TPC)
        hid = [room_d[0:D + 1, 2 * COLS + b * CHUNK:2 * COLS + (b + 1) * CHUNK] for b in range(2)]

        dst_cur = sb("dst_cur", [P, COLS], i32)
        dst_prev = sb("dst_prev", [P, COLS], i32)
        keep_sb = sb("keep_sb", [P, COLS], bf16)
        cap_sb = sb("cap_sb", [P, COLS], bf16)
        is_low = [sb(f"is_low{b}", [P, TPC, P], bf16) for b in range(2)]
        is_high = [sb(f"is_high{b}", [P, TPC, HIGHS], bf16) for b in range(2)]
        edges_of = sb("edges_of", [P, HIGHS])
        ones_sb = sb("ones_sb", [HIGHS, P])
        running = sb("running", [HIGHS, P])
        edges_before = sb("edges_before", [HIGHS, 1])
        cnt_rows = sb("cnt_rows", [HIGHS, P])
        cnt = sb("cnt", [P, NT])
        cnt_prev = sb("cnt_prev", [P, NT])
        zero_sb = sb("zero_sb", [HIGHS, 1])
        end_f = sb("end_f", [P, NT])
        end_i = sb("end_i", [P, NT], i32)
        deg = sb("deg", [P, NT])
        deg1 = sb("deg1", [P, NT])
        deg_root = sb("deg_root", [P, NT])
        mask = sb("mask", [P, NT])
        dinv = sb("dinv", [P, NT])
        mask_dinv = sb("mask_dinv", [P, NT])

        idx = [sb(f"idx{h}", [P, CPH * TPC], i32) for h in range(HALVES)]
        flags = [sb(f"flags{h}", [D, HALF], bf16) for h in range(HALVES)]
        edge_in = [sb(f"edge_in{h}", [STACK0, HALF], bf16) for h in range(HALVES)]
        split_room = sb("split_room", [P, max(AHEAD * PARTS * FLAT0, PARTS * FLAT2)], bf16)
        split0 = [split_room[:, b * PARTS * FLAT0:(b + 1) * PARTS * FLAT0].rearrange("p (n c) -> p n c", n=PARTS)
                  for b in range(AHEAD)]
        split2 = split_room[:, 0:PARTS * FLAT2].rearrange("p (n c) -> p n c", n=PARTS)
        rows = [sb(f"rows{k}", [P, TPC * D]) for k in range(SLOTS)]
        msg = [sb(f"msg{b}", [P, TPC * D]) for b in range(2)]
        scan = [sb(f"scan{k}", [D, CHUNK]) for k in range(BUFS)]
        back = [sb(f"back{k}", [P, TPC * D]) for k in range(BUFS)]

        agg = [sb(f"agg{h}", [P, GT, D]) for h in range(2)]
        aggm = [sb(f"aggm{h}", [P, GT, D]) for h in range(2)]
        relu_t = [sb(f"relu_t{h}", [D, GROUP]) for h in range(2)]
        agg_t = [sb(f"agg_t{h}", [D, GROUP]) for h in range(2)]
        new_t = sb("new_t", [D + 1, GROUP])
        y_t = agg_t
        z = sb("z", [P, GT, D])
        u = sb("u", [P, GT, D])
        y = [sb(f"y{h}", [P, GT, D]) for h in range(2)]
        stats = sb("stats", [P, GT, 6])
        mv = [sb(f"mv{h}", [P, GT, 2]) for h in range(2)]
        std = sb("std", [P, GT])
        rstd_all = sb("rstd_all", [P, NT_ROOM])
        shift_all = sb("shift_all", [P, NT_ROOM])
        new = [sb(f"new{h}", [P, GT, D]) for h in range(2)]
        tab = [sb(f"tab{h}", [P, GT, D]) for h in range(2)]
        conv_stats = sb("conv_stats", [D, 2 * GROUPS, 6])
        gn_mv = sb("gn_mv", [D, 2])
        gn = sb("gn", [D, 8])
        (G_AMEAN, G_DIFF, G_VAR, G_STD, G_RSTD, G_SCALE, G_PROD, G_SHIFT) = range(8)

        def gcol(c):
            return gn[:, c:c + 1]

        bank = [ctx.enter_context(nc.psum_tensor(f"bank{b}", [P, 512], f32)) for b in range(8)]
        ps_x = [bank[0], bank[1]]
        ps_back = [bank[2], bank[3]]
        ps_hid = bank[4]
        ps_counts, ps_before = bank[4][0:HIGHS, 0:P], bank[4][0:HIGHS, P:P + 1]
        ps_w = [bank[6], bank[7]]
        ps_t = [bank[0], bank[1]]
        ps_t2 = [bank[2], bank[3]]
        ps_z = [bank[4], bank[5]]
        ps_tab = bank[6]
        ps_tabs = [bank[6], bank[7]]
        ps_c = [[bank[6], bank[7]], [bank[4], bank[5]]]
        ps_root_t = bank[5][0:D, 0:P]
        ps_root = bank[5][:, P:P + D]
        TCUT = [(0, 4), (4, GT)]

        s_const = sem("s_const")
        s_ones = sem("s_ones")
        s_dst_in = sem("s_dst_in")
        s_flag_made = sem("s_flag_made")
        s_flag_half = sem("s_flag_half")
        s_flag_out = sem("s_flag_out")
        s_digit = sem("s_digit")
        s_one_hot = sem("s_one_hot")
        s_counted = sem("s_counted")
        s_counts_tr = sem("s_counts_tr")
        s_running = sem("s_running")
        s_before = sem("s_before")
        s_cnt = sem("s_cnt")
        s_end_f = sem("s_end_f")
        s_ends = sem("s_ends")
        s_cnt_out = sem("s_cnt_out")
        s_prev_in = sem("s_prev_in")
        s_deg = sem("s_deg")
        s_deg1 = sem("s_deg1")
        s_deg_root = sem("s_deg_root")
        s_dinv = sem("s_dinv")

        s_raw0, s_raw2 = sem("s_raw0"), sem("s_raw2")
        s_part0, s_part2 = sem("s_part0"), sem("s_part2")
        s_split0, s_split2 = sem("s_split0"), sem("s_split2")
        s_parts_out0, s_parts_out2 = sem("s_parts_out0"), sem("s_parts_out2")
        s_w_part = sem("s_w_part")
        s_w_stack = sem("s_w_stack")
        s_bias = sem("s_bias")
        s_averaged = sem("s_averaged")
        s_centred = sem("s_centred")
        s_res = sem("s_res")
        s_sum = sem("s_sum")
        s_root_in = sem("s_root_in")
        s_root_tr = sem("s_root_tr")
        s_root_ev = sem("s_root_ev")
        s_root = sem("s_root")
        s_root_out = sem("s_root_out")
        s_sum_in, s_sum_tr, s_sum_ev = sem("s_sum_in"), sem("s_sum_tr"), sem("s_sum_ev")

        s_idx = [sem(f"s_idx{h}") for h in range(HALVES)]
        s_flags = [sem(f"s_flags{h}") for h in range(HALVES)]
        s_edge = [sem(f"s_edge{h}") for h in range(HALVES)]
        s_gath = [sem(f"s_gath{k}") for k in range(SLOTS)]
        s_hid = sem("s_hid")
        s_relu = sem("s_relu")
        s_w = sem("s_w")
        s_msg = sem("s_msg")
        s_xt = sem("s_xt")
        s_scan = sem("s_scan")
        s_back = sem("s_back")
        s_evac = sem("s_evac")
        s_rows_out = [sem(f"s_rows_out{k}") for k in range(BUFS)]
        s_tally_sp, s_tally_pool, s_tally_act, s_tally_dve = (sem(f"s_tally_{e}") for e in ("sp", "pool", "act", "dve"))

        GN_STEPS = 9
        pair = {name: [sem(f"n_{name}{h}") for h in range(2)] for name in ("fetched", "new_out", "tab_out")}
        step = {name: sem("n_" + name) for name in (
            "masked", "kept", "agg_tr", "agg_ev", "z", "pre", "u", "y", "bn", "mv", "std",
            "rstd", "shift", "new", "new_tr", "new_ev", "tab", "tab_ev", "conv", "conv_ev", "conv_bn", "gn", "relu")}
        counts = {}

        class NodePhase:

            def __init__(self, conv=None, wn=None, finish=False, act=None, norm=False, out=None, table=None,
                         tmat=None, tscale=None, centred=False, rest=None, keep=None, keep_step=None, scale=None,
                         chain=(None,), made=None):
                self.conv, self.wn, self.finish, self.act, self.norm = conv, wn, finish, act, norm
                self.out, self.table, self.tmat, self.tscale, self.rest, self.scale = out, table, tmat, tscale, rest, scale
                self.has_pre, self.has_u = "pre" in chain, "u" in chain
                self.opening, self.closing = chain[0], chain[-1]
                self.made = made
                self.centred = centred
                self.keep, self.keep_step = keep, keep_step
                self.fetches = not finish
                self.masks = conv is not None
                self.transposes = conv is not None or wn is not None
                by_conv, by_mask, by_agg = GROUPS * (conv is not None), GROUPS * self.masks, GROUPS * self.transposes
                by_new = GROUPS * (norm and not centred)
                by_new_t = GROUPS * (tmat is not None and not centred)
                by_norm, by_table, rows_made = GROUPS * norm, GROUPS * (tmat is not None), out is not None
                adds = {
                    "fetched": PAIRS * self.fetches,
                    "new_out": PAIRS * rows_made, "tab_out": PAIRS * (table is not None),
                    "masked": by_mask, "agg_tr": by_agg, "agg_ev": by_agg,
                    "z": GROUPS * (finish or wn is not None), "pre": GROUPS * self.has_pre, "u": GROUPS * self.has_u,
                    "y": by_norm, "bn": by_norm, "mv": by_norm, "std": by_norm, "rstd": by_norm, "shift": by_norm,
                    "new": by_new, "new_tr": by_new_t, "new_ev": by_new_t, "kept": GROUPS * centred, "tab": by_table, "tab_ev": by_table,
                    "conv": by_conv, "conv_ev": by_conv, "conv_bn": by_conv, "gn": GN_STEPS * (conv is not None),
                    "relu": GROUPS * finish,
                }
                self.start = {name: counts.get(name, 0) for name in adds}
                for name, n in adds.items():
                    counts[name] = self.start[name] + n

            def after(self, name, n):
                return self.start[name] + n

        n0 = NodePhase(wn=M_WN_0, act="relu", norm=True, rest=rows_a, keep=rows_b, keep_step="new", out=x1,
                       chain=("pre", "y"), made="new")
        n1 = NodePhase(conv=(M_W1_1, C_B_1, C_W_1, C_G_1, C_A_1))
        f1 = NodePhase(finish=True, rest=rows_b, keep=rows_a, keep_step="u", out=h1, chain=("u",), made="u")
        n2 = NodePhase(conv=(M_W2_1, C_B_2, C_W_2, C_G_2, C_A_2))
        f2 = NodePhase(finish=True, norm=True, keep=rows_b, table=t3, tmat=M_MSG1, centred=True)
        n3 = NodePhase(act="leaky", keep=rows_a, keep_step="u", table=t4, tmat=M_MSG2, chain=("pre", "u"), made="u")
        n4 = NodePhase(act="leaky", norm=True, rest=rows_b, keep=rows_b, keep_step="y", table=t5, tmat=M_LIN, tscale=dinv,
                       chain=("pre", "u", "y"), made="new")
        n5 = NodePhase(act="relu", norm=True, rest=rows_b, keep=rows_a, keep_step="new", out=out, scale=mask_dinv,
                       chain=("pre", "y"), made="new")
        PHASES = [[n0], [n1, f1], [n2, f2], [n3], [n4], [n5]]
        ROOTS = [(rows_a, M_WS_0, False), None, None, (rows_b, M_ROOT1, True), (rows_a, M_ROOT2, False), (rows_b, M_ROOT3, True)]

        def root_start(q):
            return NT_ROOM * sum(r is not None for r in ROOTS[:q])

        def group_rows(table, g):
            return table[bass.ds(g * GROUP, GROUP), :].rearrange("(p t) d -> p t d", p=P)

        block = ctx.enter_context(nc.Block())

        @block.sync
        def _(sp):
            def edge_pass(q, kind):
                flag_row = cap_row if kind == MAX else keep_row

                def load_idx(i, h):
                    sp.dma_start(idx[h][:], src_idx[bass.ds((i - q * ITERS) * HALVES + h, 1), :, :]
                                 .rearrange("a p c -> (a p) c")).then_inc(s_idx[h], 16)

                def load_edges(i, h):
                    if kind == FILTER:
                        at = 0
                        for n in (PARTS, 2, 1):
                            sp.dma_start(edge_in[h][at:at + n * ED0, :],
                                         parts0[bass.ds(i, 1), 0:n, :, h * HALF:(h + 1) * HALF]
                                         .rearrange("a n f e -> (a n f) e")).then_inc(s_edge[h], 16)
                            at += n * ED0
                    if kind == MAX:
                        sp.dma_start(edge_in[h][0:STACK2, :],
                                     parts2[bass.ds(i - q * ITERS, 1), :, :, h * HALF:(h + 1) * HALF]
                                     .rearrange("a n f e -> (a n f) e")).then_inc(s_edge[h], 16)

                def load_raw0(i, b):
                    sp.dma_start(raw0[b][:], ea17[bass.ds(i, 1), :].rearrange("a (p c) -> (a p) c", p=P)).then_inc(s_raw0, 16)

                def store_parts0(i, b):
                    sp.wait_ge(s_split0, i + 1)
                    settle(sp, s_tally_sp)
                    sp.dma_start(parts0[bass.ds(i, 1)].rearrange("a n f e -> (a n f e)").rearrange("(n p c) -> p n c", n=PARTS, p=P),
                                 split0[b][:]).then_inc(s_parts_out0, 16)

                def load_raw2(i):
                    sp.dma_start(raw2[:], ea32[bass.ds(i, 1), :].rearrange("a (p c) -> (a p) c", p=P)).then_inc(s_raw2, 16)

                def store_parts2(i):
                    sp.wait_ge(s_split2, i + 1)
                    settle(sp, s_tally_sp)
                    sp.dma_start(parts2[bass.ds(i, 1)].rearrange("a n f e -> (a n f e)").rearrange("(n p c) -> p n c", n=PARTS, p=P),
                                 split2[:]).then_inc(s_parts_out2, 16)

                def load_flags(i, h):
                    e0 = ((i - q * ITERS) * HALVES + h) * HALF
                    sp.dma_start(flags[h][:], flag_row[:, bass.ds(e0, HALF)].to_broadcast([D, HALF])).then_inc(s_flags[h], 16)

                def load_half(i, h):
                    load_idx_behind(i, h)
                    at_least(sp, s_scan, (i - 1) * SLOTS + (h + 1) * CPH)
                    settle(sp, s_tally_sp)
                    load_edges(i, h)
                    load_flags(i, h)

                def load_idx_behind(i, h):
                    i, h = (i, h + 1) if h + 1 < HALVES else (i + 1, 0)
                    for k in range(h * CPH, (h + 1) * CPH):
                        at_least(sp, s_gath[k], 16 * TPC * i)
                    settle(sp, s_tally_sp)
                    load_idx(i, h)

                if q == 0:
                    for h in range(HALVES):
                        load_idx(0, h)
                    for b in range(AHEAD):
                        load_raw0(b, b)
                    sp.dma_start(dst_cur[:], dst_shifted[1:EP + 1, :].rearrange("(p c) a -> p (c a)", p=P)).then_inc(s_dst_in, 16)
                    sp.dma_start(dst_prev[:], dst_shifted[0:EP, :].rearrange("(p c) a -> p (c a)", p=P)).then_inc(s_dst_in, 16)
                    for dst_sb, src_dram in ((mats_sb, mats), (cols_sb, cols), (edge_w_sb, edge_w), (part_of_sb, part_of),
                                             (eye_sb, eye), (digits_sb, digits), (lower_sb, lower)):
                        sp.dma_start(dst_sb[:], src_dram).then_inc(s_const, 16)
                    sp.dma_start(rows_a[:, 0:NT, :].rearrange("p (g t) d -> p g (t d)", t=GT),
                                 x.rearrange("(g p t) d -> p g (t d)", p=P, t=GT)).then_inc(s_res, 16)
                    for b in range(AHEAD):
                        store_parts0(b, b)
                    load_raw0(AHEAD, 0)
                    sp.wait_ge(s_parts_out0, 16 * AHEAD)
                    for h in range(HALVES):
                        load_edges(0, h)
                    sp.wait_ge(s_flag_made, 1)
                    sp.dma_start(keep_row.rearrange("a (p c) -> (a p) c", p=P), keep_sb[:]).then_inc(s_flag_out, 16)
                    sp.wait_ge(s_flag_made, 3)
                    sp.dma_start(cap_row.rearrange("a (p c) -> (a p) c", p=P), cap_sb[:]).then_inc(s_flag_out, 16)
                    sp.wait_ge(s_flag_out, 32)
                    for h in range(HALVES):
                        load_flags(0, h)
                    load_idx_behind(0, HALVES - 1)
                else:
                    for h in range(HALVES):
                        load_half(q * ITERS, h)
                    if q == 1:
                        load_raw2(0)
                with sp.Fori(q * ITERS + 1, (q + 1) * ITERS) as i:
                    if q == 0:
                        sp.wait_ge(s_parts_out0, 16 * i + 16)
                        settle(sp, s_tally_sp)
                    for h in range(HALVES):
                        load_half(i, h)
                    if q == 0:
                        store_parts0(i + 1, 0)
                        load_raw0(i + AHEAD, 0)
                    if q == 1:
                        store_parts2(i - 1 - q * ITERS)
                        load_raw2(i - q * ITERS)
                if q == 1:
                    store_parts2(ITERS - 1)
                    sp.wait_ge(s_parts_out2, 16 * ITERS)

            def counts_shifted():
                sp.dma_start(cnt_row[:, 0:1], zero_sb[0:1, :]).then_inc(s_cnt_out, 16)
                sp.wait_ge(s_cnt, 1)
                sp.dma_start(cnt_row[0, 1:1 + NP].rearrange("(h l) -> h l", l=P), cnt_rows[:]).then_inc(s_cnt_out, 16)
                sp.wait_ge(s_cnt_out, 32)
                for target, first in ((cnt, 1), (cnt_prev, 0)):
                    sp.dma_start(target[:].rearrange("p (g t) -> p g t", t=GT),
                                 cnt_row[0, first:first + NP].rearrange("(g p t) -> p g t", p=P, t=GT)).then_inc(s_prev_in, 16)

            def node_phase(ph):
                def one(g, j, h):
                    if ph.out is not None and within(g - 1):
                        _, b = earlier(j, h, 1)
                        sp.wait_ge(step[ph.made], ph.after(ph.made, g))
                        settle(sp, s_tally_sp)
                        sp.dma_start(group_rows(ph.out, g - 1),
                                     ph.keep[:, bass.ds((g - 1) * GT, GT), :].rearrange("p t d -> p (t d)")
                                     ).then_inc(pair["new_out"][b], 16)
                    if ph.table is not None and within(g - 2):
                        sp.wait_ge(step["tab_ev"], ph.after("tab_ev", g - 1))
                        sp.dma_start(group_rows(ph.table, g - 2), tab[h][:]).then_inc(pair["tab_out"][h], 16)

                over_groups(sp, one)
                for h in range(2):
                    if ph.out is not None:
                        sp.wait_ge(pair["new_out"][h], 16 * ph.after("new_out", PAIRS))
                    if ph.table is not None:
                        sp.wait_ge(pair["tab_out"][h], 16 * ph.after("tab_out", PAIRS))

            for q, kind in enumerate(PASSES):
                edge_pass(q, kind)
                if q == 0:
                    counts_shifted()
                for ph in PHASES[q]:
                    if ph.conv is None:
                        node_phase(ph)

        @block.gpsimd
        def _(pool):
            def edge_pass(q, kind):
                def gather_chunk(i, k):
                    h = k // CPH
                    pool.wait_ge(s_idx[h], 16 * i + 16)
                    at_least(pool, s_xt, (i - 1) * SLOTS + k + 1)
                    settle(pool, s_tally_pool)
                    for j in range(TPC):
                        c = (k % CPH) * TPC + j
                        pool.indirect_dma_start(rows[k][:, j * D:(j + 1) * D], None, tables[q],
                                                bass.IndirectOffsetOnAxis(ap=idx[h][:, c:c + 1], axis=0)).then_inc(s_gath[k], 16)

                def iteration(i):
                    for k in range(SLOTS):
                        gather_chunk(i, k)

                iteration(q * ITERS)
                with pool.Fori(q * ITERS + 1, (q + 1) * ITERS) as i:
                    iteration(i)

            def fetch(q, ph):
                for k in range(BUFS):
                    pool.wait_ge(s_rows_out[k], 16 * (q + 1) * ITERS * ROUNDS)
                if q == 0:
                    pool.wait_ge(s_ends, 1)
                taken = "masked" if ph.masks else "agg_tr" if ph.transposes else "pre"
                for g in range(GROUPS):
                    if g >= 2:
                        pool.wait_ge(step[taken], ph.after(taken, g - 1))
                    for t in range(GT):
                        pool.indirect_dma_start(agg[g % 2][:, t, :], None, scan_rows,
                                                bass.IndirectOffsetOnAxis(ap=end_i[:, g * GT + t:g * GT + t + 1], axis=0)
                                                ).then_inc(pair["fetched"][g % 2], 16)

            for q, kind in enumerate(PASSES):
                edge_pass(q, kind)
                fetch(q, PHASES[q][0])
                last = PHASES[q][-1]
                table = "tab_out" if last.table is not None else "new_out"
                for h in range(2):
                    pool.wait_ge(pair[table][h], 16 * last.after(table, PAIRS))

        @block.tensor
        def _(pe):
            def edge_pass(q, kind):
                def hidden(i, k):
                    n, h = i * SLOTS + k, k // CPH
                    lo = (k % CPH) * CHUNK
                    pe.wait_ge(s_edge[h], 16 * PARTS * (i + 1))
                    at_least(pe, s_relu, n)
                    nc.tensor.matmul(ps_hid[0:D, :], w_stack[:], edge_in[h][:, lo:lo + CHUNK],
                                     start=True, stop=True).then_inc(s_hid, 1)

                def filters(i, k):
                    n, b = i * SLOTS + k, k % 2
                    pe.wait_ge(s_relu, n + 1)
                    pe.wait_ge(s_one_hot, n + 1)
                    at_least(pe, s_msg, n - 1)
                    for j in range(TPC):
                        nc.tensor.matmul(ps_w[b][:, TPC * D:TPC * D + HIGHS], is_low[b][:, j, :], is_high[b][:, j, :],
                                         start=(j == 0), stop=(j == TPC - 1))
                    for j in range(TPC):
                        m = nc.tensor.matmul(ps_w[b][:, j * D:(j + 1) * D], hid[b][:, j::TPC], mat(M_W2_0), start=True, stop=True)
                    m.then_inc(s_w, 1)

                def forward(i, k):
                    n, h, b = i * SLOTS + k, k // CPH, k % 2
                    lo = (k % CPH) * CHUNK
                    if kind == FILTER:
                        pe.wait_ge(s_msg, n + 1)
                    else:
                        pe.wait_ge(s_gath[k], 16 * TPC * (i + 1))
                    at_least(pe, s_scan, n - 1)
                    source = msg[b] if kind == FILTER else rows[k]
                    if kind == MAX:
                        pe.wait_ge(s_edge[h], 16 * (i + 1))
                        for part in range(PARTS):
                            n_rows = (PARTS - part) * ED2
                            nc.tensor.matmul(ps_x[b][0:D, :], w_parts[0:n_rows, part, (q - 2) * D:(q - 1) * D],
                                             edge_in[h][0:n_rows, lo:lo + CHUNK], start=(part == 0), stop=False)
                        for j in range(TPC):
                            m = nc.tensor.matmul(ps_x[b][0:D, j::TPC], source[:, j * D:(j + 1) * D], eye_sb[:],
                                                 start=False, stop=(j == TPC - 1))
                    else:
                        for j in range(TPC):
                            m = nc.tensor.transpose(ps_x[b][0:D, j::TPC], source[:, j * D:(j + 1) * D], eye_sb[:])
                    m.then_inc(s_xt, 1)

                def backward(i, k):
                    n, b = i * SLOTS + k, k % 2
                    pe.wait_ge(s_scan, n + 1)
                    at_least(pe, s_evac, n - 1)
                    for j in range(TPC):
                        m = nc.tensor.transpose(ps_back[b][:, j * D:(j + 1) * D], scan[k % BUFS][:, j::TPC], eye_sb[0:D, 0:D])
                    m.then_inc(s_back, 1)

                def root_step(i, k):
                    m, at = k // 4, k % 4
                    n = root_start(q) + ROOT_SLOTS * (i - q * ITERS) + m
                    if at == 1:
                        pe.wait_ge(s_root_in, n + 1)
                        at_least(pe, s_root_out, n)
                        nc.tensor.transpose(ps_root_t, root_in[:], eye_sb[:]).then_inc(s_root_tr, 1)
                    if at == 3:
                        pe.wait_ge(s_root_ev, n + 1)
                        nc.tensor.matmul(ps_root, root_t[:], mat(ROOTS[q][1]), start=True, stop=True).then_inc(s_root, 1)

                def sum_step(i, k):
                    n = ROOT_SLOTS * (i - q * ITERS) + k // 4
                    if k % 4 == 1:
                        pe.wait_ge(s_sum_in, n + 1)
                        at_least(pe, s_sum_ev, n)
                        nc.tensor.transpose(ps_root_t, root_in[:], eye_sb[:]).then_inc(s_sum_tr, 1)

                def chunk(i, k, behind):
                    if kind == FILTER:
                        hidden(i, k)
                        if behind >= 1:
                            filters(*before(i, k, 1))
                        if behind >= 2:
                            forward(*before(i, k, 2))
                        if behind >= 3:
                            backward(*before(i, k, 3))
                    else:
                        forward(i, k)
                        if behind >= 1:
                            backward(*before(i, k, 1))
                    if ROOTS[q] is not None:
                        root_step(i, k)
                    if q == 2:
                        sum_step(i, k)

                first, last = q * ITERS, (q + 1) * ITERS - 1
                for k in range(SLOTS):
                    chunk(first, k, k)
                with pe.Fori(first + 1, last + 1) as i:
                    for k in range(SLOTS):
                        chunk(i, k, SLOTS)
                if kind == FILTER:
                    filters(last, SLOTS - 1)
                    forward(last, SLOTS - 2)
                    backward(last, SLOTS - 3)
                    forward(last, SLOTS - 1)
                    pe.wait_ge(s_counted, ITERS * SLOTS)
                    pe.wait_ge(s_relu, ITERS * SLOTS)
                    nc.tensor.transpose(ps_counts, edges_of[:], eye_sb[:]).then_inc(s_counts_tr, 1)
                    backward(last, SLOTS - 2)
                backward(last, SLOTS - 1)
                if kind == FILTER:
                    pe.wait_ge(s_running, 1)
                    nc.tensor.matmul(ps_before, lower_sb[:], running[:, P - 1:P], start=True, stop=True).then_inc(s_before, 1)

            def transpose_tiles(dst, src, semaphore):
                for b, (a, e) in enumerate(TCUT):
                    for t in range(a, e):
                        m = nc.tensor.transpose(dst[b][0:D, (t - a) * P:(t - a + 1) * P], src[:, t, :], eye_sb[:])
                m.then_inc(semaphore, 1)

            def conv_phase(ph):
                def one(g, j, h):
                    if within(g):
                        pe.wait_ge(step["masked"], ph.after("masked", g + 1))
                        at_least(pe, step["agg_ev"], ph.after("agg_ev", g))
                        transpose_tiles(ps_t, aggm[h], step["agg_tr"])
                    if within(g - 1):
                        _, b = earlier(j, h, 1)
                        pe.wait_ge(step["agg_ev"], ph.after("agg_ev", g))
                        at_least(pe, step["conv_ev"], ph.after("conv_ev", g - 2))
                        for c in range(2):
                            m = nc.tensor.matmul(ps_c[b][c][0:D, 0:GROUP // 2], mat(ph.conv[0])[0:D, :],
                                                 agg_t[b][0:D, c * GROUP // 2:(c + 1) * GROUP // 2], start=True, stop=True)
                        m.then_inc(step["conv"], 1)
                over_groups(pe, one)

            def centred_phase(ph):
                def one(g, j, h):
                    if within(g):
                        pe.wait_ge(step["y"], ph.after("y", g + 1))
                        at_least(pe, step["kept"], ph.after("kept", g - 1))
                        for t in range(GT):
                            m = nc.tensor.transpose(ps_z[h][:, t * D:(t + 1) * D], y_t[h][:, t * P:(t + 1) * P], eye_sb[0:D, 0:D])
                        m.then_inc(step["z"], 1)
                        at_least(pe, step["tab_ev"], ph.after("tab_ev", g - 1))
                        for t in range(GT):
                            m = nc.tensor.matmul(ps_tabs[h][:, t * D:(t + 1) * D], y_t[h][:, t * P:(t + 1) * P], w_centred[:],
                                                 start=True, stop=True)
                        m.then_inc(step["tab"], 1)
                over_groups(pe, one)

            def node_phase(ph):
                def one(g, j, h):
                    _, b = earlier(j, h, 1)
                    if ph.tmat is not None and within(g - 2):
                        pe.wait_ge(step[ph.made], ph.after(ph.made, g - 1))
                        at_least(pe, step["new_ev"], ph.after("new_ev", g - 2))
                        transpose_tiles(ps_t2, new[h], step["new_tr"])
                    if ph.wn is not None and within(g - 1):
                        at_least(pe, step[ph.opening], ph.after(ph.opening, g - 2))
                        pe.wait_ge(step["agg_ev"], ph.after("agg_ev", g))
                        for t in range(GT):
                            m = nc.tensor.matmul(ps_z[b][:, t * D:(t + 1) * D], agg_t[b][:, t * P:(t + 1) * P],
                                                 mat(ph.wn)[0:D, :], start=True, stop=True)
                        m.then_inc(step["z"], 1)
                    if ph.wn is not None and within(g):
                        pe.wait_ge(pair["fetched"][h], 16 * GT * ph.after("fetched", j + 1))
                        at_least(pe, step["agg_ev"], ph.after("agg_ev", g))
                        transpose_tiles(ps_t, agg[h], step["agg_tr"])
                    if ph.tmat is not None and within(g - 2):
                        pe.wait_ge(step["new_ev"], ph.after("new_ev", g - 1))
                        at_least(pe, step["tab_ev"], ph.after("tab_ev", g - 2))
                        for t in range(GT):
                            m = nc.tensor.matmul(ps_tab[:, t * D:(t + 1) * D], new_t[:, t * P:(t + 1) * P], mat(ph.tmat),
                                                 start=True, stop=True)
                        m.then_inc(step["tab"], 1)
                    if ph.finish and within(g):
                        pe.wait_ge(step["relu"], ph.after("relu", g + 1))
                        at_least(pe, step[ph.opening], ph.after(ph.opening, g - 1))
                        for t in range(GT):
                            m = nc.tensor.transpose(ps_z[h][:, t * D:(t + 1) * D], relu_t[h][:, t::GT], eye_sb[0:D, 0:D])
                        m.then_inc(step["z"], 1)
                if ph.finish or ph.wn is not None or ph.tmat is not None:
                    over_groups(pe, one)

            pe.wait_ge(s_const, 112)
            pe.wait_ge(s_ones, 1)
            nc.tensor.matmul(bank[0][0:D, 0:D], averaging[:], mat(M_MSG1)[0:D, :], start=True, stop=True).then_inc(s_averaged, 1)
            pe.wait_ge(s_bias, 1)
            pe.wait_ge(s_centred, 1)
            pe.wait_ge(s_w_stack, PARTS)
            for q, kind in enumerate(PASSES):
                edge_pass(q, kind)
                for ph in PHASES[q]:
                    if ph.conv is not None:
                        conv_phase(ph)
                    elif ph.centred:
                        centred_phase(ph)
                    else:
                        node_phase(ph)

        @block.scalar
        def _(act):
            def edge_pass(q, kind):
                def hidden(i, k):
                    n, b = i * SLOTS + k, k % 2
                    act.wait_ge(s_hid, n + 1)
                    at_least(act, s_w, n - 1)
                    nc.scalar.activation(hid[b][0:D, :], ps_hid[0:D, :], ACT.Relu, bias=col(C_B1_0)).then_inc(s_relu, 1)

                def backward(i, k):
                    n, b, m = i * SLOTS + k, k % 2, k % BUFS
                    act.wait_ge(s_back, n + 1)
                    at_least(act, s_rows_out[m], 16 * (i * ROUNDS + k // BUFS))
                    nc.scalar.activation(back[m][:], ps_back[b][:, 0:TPC * D], ACT.Copy).then_inc(s_evac, 1)
                    act.wait_ge(s_evac, n + 1)
                    e0 = (i - q * ITERS) * STEP + k * CHUNK
                    act.dma_start(scan_rows[bass.ds(e0, CHUNK), :].rearrange("(p j) d -> p (j d)", p=P), back[m][:]
                                  ).then_inc(s_rows_out[m], 16)

                def root_step(i, k):
                    m, at = k // 4, k % 4
                    rows_of, _, norm_due = ROOTS[q]
                    tile = ROOT_SLOTS * (i - q * ITERS) + m
                    n = root_start(q) + tile
                    here = rows_of[:, bass.ds(tile, 1), :].rearrange("p a d -> p (a d)")
                    if at == 0:
                        if norm_due:
                            scale, bias = rstd_all[:, bass.ds(tile, 1)], shift_all[:, bass.ds(tile, 1)]
                            nc.scalar.activation(root_in[:], here, ACT.Identity, bias=bias, scale=scale).then_inc(s_root_in, 1)
                            act.wait_ge(s_root_in, n + 1)
                            settle(act, s_tally_act)
                            nc.scalar.activation(here, here, ACT.Identity, bias=bias, scale=scale)
                        else:
                            nc.scalar.activation(root_in[:], here, ACT.Copy).then_inc(s_root_in, 1)
                    if at == 2:
                        act.wait_ge(s_root_tr, n + 1)
                        nc.scalar.activation(root_t[0:D, :], ps_root_t, ACT.Copy).then_inc(s_root_ev, 1)
                    if at == 3:
                        act.wait_ge(s_root, n + 1)
                        settle(act, s_tally_act)
                        nc.scalar.activation(root_all[:, bass.ds(tile, 1), :].rearrange("p a d -> p (a d)"), ps_root, ACT.Copy
                                             ).then_inc(s_root_out, 1)

                def sum_step(i, k):
                    n = ROOT_SLOTS * (i - q * ITERS) + k // 4
                    if k % 4 == 0:
                        nc.scalar.activation(root_in[:], rows_a[:, bass.ds(n, 1), :].rearrange("p a d -> p (a d)"), ACT.Copy
                                             ).then_inc(s_sum_in, 1)
                    if k % 4 == 2:
                        act.wait_ge(s_sum_tr, n + 1)
                        settle(act, s_tally_act)
                        nc.scalar.activation(sum_t[:, bass.ds(n * P, P)], ps_root_t, ACT.Copy).then_inc(s_sum_ev, 1)

                lag = 3 if kind == FILTER else 1

                def chunk(i, k, behind):
                    if kind == FILTER:
                        hidden(i, k)
                    if behind >= lag:
                        backward(*before(i, k, lag))
                    if ROOTS[q] is not None:
                        root_step(i, k)
                    if q == 2:
                        sum_step(i, k)

                first, last = q * ITERS, (q + 1) * ITERS - 1
                if q == 0:
                    act.wait_ge(s_res, 16)
                if q == 2:
                    act.wait_ge(s_sum, 1)
                for k in range(SLOTS):
                    chunk(first, k, k)
                with act.Fori(first + 1, last + 1) as i:
                    for k in range(SLOTS):
                        chunk(i, k, SLOTS)
                for k in range(SLOTS - lag, SLOTS):
                    backward(last, k)

            def evacuate(dst, banks, semaphore):
                for b, (a, e) in enumerate(TCUT):
                    m = nc.scalar.activation(dst[0:D, a * P:e * P], banks[b][0:D, 0:(e - a) * P], ACT.Copy)
                m.then_inc(semaphore, 1)

            def conv_phase(ph):
                def one(g, j, h):
                    if within(g):
                        act.wait_ge(step["agg_tr"], ph.after("agg_tr", g + 1))
                        at_least(act, step["conv"], ph.after("conv", g - 1))
                        for b, (a, e) in enumerate(TCUT):
                            m = nc.scalar.activation(agg_t[h][0:D, :].rearrange("d (p t) -> d t p", t=GT)[:, a:e, :],
                                                     ps_t[b][0:D, 0:(e - a) * P].rearrange("d (t p) -> d t p", p=P), ACT.Copy)
                        m.then_inc(step["agg_ev"], 1)
                    if within(g - 1):
                        _, b = earlier(j, h, 1)
                        act.wait_ge(step["conv"], ph.after("conv", g))
                        for c in range(2):
                            m = nc.scalar.activation(conv[:, bass.ds((g - 1) * GROUP + c * (GROUP // 2), GROUP // 2)],
                                                     ps_c[b][c][0:D, 0:GROUP // 2], ACT.Identity, bias=col(ph.conv[1]))
                        m.then_inc(step["conv_ev"], 1)
                over_groups(act, one)
                act.wait_ge(step["gn"], ph.after("gn", 4))
                nc.scalar.activation(gcol(G_STD), gcol(G_VAR), ACT.Sqrt, bias=eps_sb[0:D, :]).then_inc(step["gn"], 1)
                act.wait_ge(step["gn"], ph.after("gn", GN_STEPS))

            def centred_phase(ph):
                def one(g, j, h):
                    if within(g):
                        at_least(act, step["y"], ph.after("y", g - 1))
                        nc.scalar.activation(relu_t[h][:], conv[:, bass.ds(g * GROUP, GROUP)], ACT.Relu,
                                             bias=gcol(G_SHIFT), scale=gcol(G_SCALE)).then_inc(step["relu"], 1)
                    if within(g - 2):
                        act.wait_ge(step["tab"], ph.after("tab", g - 1))
                        act.wait_ge(step["rstd"], ph.after("rstd", g - 1))
                        at_least(act, pair["tab_out"][h], 16 * ph.after("tab_out", j - 1))
                        settle(act, s_tally_act)
                        for t in range(GT):
                            m = nc.scalar.activation(tab[h][:, t, :], ps_tabs[h][:, t * D:(t + 1) * D], ACT.Copy,
                                                     scale=rstd_all[:, bass.ds((g - 2) * GT + t, 1)])
                        m.then_inc(step["tab_ev"], 1)
                    if within(g - 1):
                        _, b = earlier(j, h, 1)
                        act.wait_ge(step["mv"], ph.after("mv", g))
                        at_least(act, step["rstd"], ph.after("rstd", g - 1))
                        nc.scalar.activation(std[:], mv[b][:, :, 1], ACT.Sqrt, bias=eps_sb[:]).then_inc(step["std"], 1)
                over_groups(act, one)
                act.wait_ge(step["shift"], ph.after("shift", GROUPS))

            def node_phase(ph):
                def one(g, j, h):
                    if ph.wn is not None and within(g):
                        act.wait_ge(step["agg_tr"], ph.after("agg_tr", g + 1))
                        at_least(act, step["z"], ph.after("z", g - 1))
                        evacuate(agg_t[h], ps_t, step["agg_ev"])
                    if ph.norm and within(g - 1):
                        _, b = earlier(j, h, 1)
                        act.wait_ge(step["mv"], ph.after("mv", g))
                        at_least(act, step["rstd"], ph.after("rstd", g - 1))
                        nc.scalar.activation(std[:], mv[b][:, :, 1], ACT.Sqrt, bias=eps_sb[:]).then_inc(step["std"], 1)
                    if ph.finish and within(g):
                        at_least(act, step["z"], ph.after("z", g - 1))
                        nc.scalar.activation(relu_t[h][:], conv[:, bass.ds(g * GROUP, GROUP)], ACT.Relu,
                                             bias=gcol(G_SHIFT), scale=gcol(G_SCALE)).then_inc(step["relu"], 1)
                    if ph.tmat is not None and within(g - 2):
                        act.wait_ge(step["new_tr"], ph.after("new_tr", g - 1))
                        at_least(act, step["tab"], ph.after("tab", g - 2))
                        evacuate(new_t, ps_t2, step["new_ev"])
                    if ph.norm and within(g - 1):
                        act.wait_ge(step["shift"], ph.after("shift", g))
                        if ph.tmat is not None:
                            at_least(act, step["new_tr"], ph.after("new_tr", g - 2))
                        settle(act, s_tally_act)
                        for t in range(GT):
                            n = bass.ds((g - 1) * GT + t, 1)
                            target = ph.keep[:, n, :].rearrange("p a d -> p (a d)") if ph.keep_step == "new" else new[b][:, t, :]
                            source = ph.keep[:, n, :].rearrange("p a d -> p (a d)") if ph.keep_step == "y" else y[b][:, t, :]
                            m = nc.scalar.activation(target, source, ACT.Identity, bias=shift_all[:, n], scale=rstd_all[:, n])
                        m.then_inc(step["new"], 1)
                    if ph.tmat is not None and within(g - 2):
                        act.wait_ge(step["tab"], ph.after("tab", g - 1))
                        at_least(act, pair["tab_out"][h], 16 * ph.after("tab_out", j - 1))
                        if ph.tscale is not None:
                            settle(act, s_tally_act)
                            for t in range(GT):
                                m = nc.scalar.activation(tab[h][:, t, :], ps_tab[:, t * D:(t + 1) * D], ACT.Copy,
                                                         scale=ph.tscale[:, bass.ds((g - 2) * GT + t, 1)])
                        else:
                            m = nc.scalar.activation(tab[h][:].rearrange("p t d -> p (t d)"), ps_tab[:, 0:GT * D], ACT.Copy)
                        m.then_inc(step["tab_ev"], 1)
                over_groups(act, one)
                if ph.norm and ph.keep_step == "y":
                    act.wait_ge(step["shift"], ph.after("shift", GROUPS))

            act.wait_ge(s_const, 112)
            act.wait_ge(s_ones, 1)
            for q, kind in enumerate(PASSES):
                edge_pass(q, kind)
                if q == 0:
                    act.wait_ge(s_deg1, 1)
                    nc.scalar.activation(deg_root[:], deg1[:], ACT.Sqrt).then_inc(s_deg_root, 1)
                for ph in PHASES[q]:
                    if ph.conv is not None:
                        conv_phase(ph)
                    elif ph.centred:
                        centred_phase(ph)
                    else:
                        node_phase(ph)

        @block.vector
        def _(dve):
            def make_flags():
                dve.wait_ge(s_dst_in, 32)
                nc.vector.tensor_tensor(keep_sb[:], dst_cur[:], dst_prev[:], ALU.is_equal).then_inc(s_flag_made, 1)
                nc.vector.tensor_copy(dst_cur_f[:], dst_cur[:]).then_inc(s_flag_made, 1)
                dve.wait_ge(s_flag_made, 2)
                nc.vector.tensor_scalar(cap_half[:], keep_sb[:], -0.5, BF16_MAX, ALU.add, ALU.mult).then_inc(s_flag_half, 1)
                dve.wait_ge(s_flag_half, 1)
                nc.vector.tensor_scalar(cap_sb[:], cap_half[:], 2.0, None, ALU.mult).then_inc(s_flag_made, 1)
                for t in (zero_sb[:], edges_of[:]):
                    nc.vector.memset(t, 0.0)
                nc.vector.memset(ones_sb[:], 1.0)
                nc.vector.memset(scan[BUFS - 1][:], 0.0)
                for t in (rows_a[:, NT:NT_ROOM, :], rows_b[:, NT:NT_ROOM, :], rstd_all[:, NT:NT_ROOM], shift_all[:, NT:NT_ROOM]):
                    nc.vector.memset(t, 0.0)
                nc.vector.memset(eps_sb[:], EPS)
                nc.vector.memset(averaging[:], 1.0 / D)
                for t in (new_t, root_t, *hid):
                    m = nc.vector.memset(t[D:D + 1, :], 1.0)
                m.then_inc(s_ones, 1)
                dve.wait_ge(s_ones, 1)
                dve.wait_ge(s_const, 112)

            def make_digits():
                nc.vector.tensor_scalar(low[:], dst_cur_f[:], 1.0 / P, -(P - 0.5) / (2 * P), ALU.mult, ALU.add).then_inc(s_digit, 1)
                dve.wait_ge(s_digit, 1)
                nc.vector.tensor_scalar(high[:], low[:], NO_FRACTION, None, ALU.add).then_inc(s_digit, 1)
                dve.wait_ge(s_digit, 2)
                nc.vector.tensor_scalar(high[:], high[:], -NO_FRACTION, None, ALU.add).then_inc(s_digit, 1)
                dve.wait_ge(s_digit, 3)
                nc.vector.scalar_tensor_tensor(out=low[:], in0=high[:], scalar=-float(P), in1=dst_cur_f[:],
                                               op0=ALU.mult, op1=ALU.add).then_inc(s_digit, 1)
                dve.wait_ge(s_digit, 4)

            def prepare_weights():
                nc.vector.tensor_tensor(mat(M_WS_0)[D:D + 1, :], mat(M_WS_0)[D:D + 1, :], mat(M_WN_0)[D:D + 1, :], ALU.add
                                        ).then_inc(s_bias, 1)
                dve.wait_ge(s_averaged, 1)
                nc.vector.tensor_tensor(w_centred[:], mat(M_MSG1)[0:D, :], bank[0][0:D, 0:D], ALU.subtract).then_inc(s_centred, 1)

            def split_weights():
                nc.vector.tensor_copy(w_parts[:, 0, :], edge_w_sb[:]).then_inc(s_w_part, 1)
                dve.wait_ge(s_w_part, 1)
                nc.vector.tensor_tensor(w_rest[:], edge_w_sb[:], w_parts[:, 0, :], ALU.subtract).then_inc(s_w_part, 1)
                dve.wait_ge(s_w_part, 2)
                nc.vector.tensor_copy(w_parts[:, 1, :], w_rest[:]).then_inc(s_w_part, 1)
                dve.wait_ge(s_w_part, 3)
                nc.vector.tensor_tensor(w_parts[:, 2, :], w_rest[:], w_parts[:, 1, :], ALU.subtract).then_inc(s_w_part, 1)
                dve.wait_ge(s_w_part, 4)
                nc.vector.tensor_scalar(w_stack[:], w_parts[:, 0, 0:D], part_of_sb[:, 0:1], None, ALU.mult).then_inc(s_w_stack, 1)
                for n in range(1, PARTS):
                    dve.wait_ge(s_w_stack, n)
                    nc.vector.scalar_tensor_tensor(out=w_stack[:], in0=w_parts[:, n, 0:D], scalar=part_of_sb[:, n:n + 1],
                                                   in1=w_stack[:], op0=ALU.mult, op1=ALU.add).then_inc(s_w_stack, 1)

            def split(raw, rest, parts, i, steps, made):
                nc.vector.tensor_copy(parts[:, 0, :], raw[:]).then_inc(steps, 1)
                dve.wait_ge(steps, 3 * i + 1)
                nc.vector.tensor_tensor(rest[:], raw[:], parts[:, 0, :], ALU.subtract).then_inc(steps, 1)
                dve.wait_ge(steps, 3 * i + 2)
                nc.vector.tensor_scalar(parts[:, 1, :], rest[:], 1.0, None, ALU.mult).then_inc(steps, 1)
                dve.wait_ge(steps, 3 * i + 3)
                nc.vector.tensor_tensor(parts[:, 2, :], rest[:], parts[:, 1, :], ALU.subtract).then_inc(made, 1)
                dve.wait_ge(made, i + 1)

            def split_layer0(i, b):
                dve.wait_ge(s_raw0, 16 * max(i + 1, AHEAD) if isinstance(i, int) else 16 * (i + 1))
                if not isinstance(i, int) or i >= AHEAD:
                    dve.wait_ge(s_parts_out0, 16 * i)
                split(raw0[b], rest0, split0[b], i, s_part0, s_split0)

            def split_layer2(i):
                dve.wait_ge(s_raw2, 16 * i + 16)
                if isinstance(i, int):
                    dve.wait_ge(s_parts_out0, 16 * (ITERS + 1))
                at_least(dve, s_parts_out2, 16 * i)
                split(raw2, rest2, split2, i, s_part2, s_split2)

            def one_hot(i, k):
                n, b = i * SLOTS + k, k % 2
                at_least(dve, s_w, n - 1)
                settle(dve, s_tally_dve)
                share = bass.ds(n * TPC, TPC)
                nc.vector.tensor_tensor(is_low[b][:], low[:, share].unsqueeze(2).to_broadcast([P, TPC, P]), all_lows, ALU.is_equal)
                nc.vector.tensor_tensor(is_high[b][:], high[:, share].unsqueeze(2).to_broadcast([P, TPC, HIGHS]), all_highs,
                                        ALU.is_equal).then_inc(s_one_hot, 1)

            def make_counts():
                dve.wait_ge(s_counts_tr, 1)
                nc.vector.tensor_tensor_scan(out=running[:], data0=ones_sb[:], data1=ps_counts, initial=zero_sb[:],
                                             op0=ALU.mult, op1=ALU.add).then_inc(s_running, 1)
                dve.wait_ge(s_before, 1)
                nc.vector.tensor_copy(edges_before[:], ps_before).then_inc(s_before, 1)
                dve.wait_ge(s_before, 2)
                nc.vector.tensor_scalar(cnt_rows[:], running[:], edges_before[:], None, ALU.add).then_inc(s_cnt, 1)

            def make_ends():
                dve.wait_ge(s_prev_in, 32)
                nc.vector.tensor_scalar(end_f[:], cnt[:], -1.0, 0.0, ALU.add, ALU.max).then_inc(s_end_f, 1)
                dve.wait_ge(s_end_f, 1)
                nc.vector.tensor_copy(end_i[:], end_f[:]).then_inc(s_ends, 1)
                nc.vector.tensor_tensor(deg[:], cnt[:], cnt_prev[:], ALU.subtract).then_inc(s_deg, 1)
                dve.wait_ge(s_deg, 1)
                nc.vector.tensor_scalar(deg1[:], deg[:], 1.0, None, ALU.max).then_inc(s_deg1, 1)
                nc.vector.tensor_scalar(mask[:], deg[:], 1.0, None, ALU.min)
                dve.wait_ge(s_deg_root, 1)
                nc.vector.reciprocal(dinv[:], deg_root[:]).then_inc(s_dinv, 1)
                dve.wait_ge(s_dinv, 1)
                nc.vector.tensor_tensor(mask_dinv[:], mask[:], dinv[:], ALU.mult).then_inc(s_dinv, 1)
                dve.wait_ge(s_dinv, 2)

            def edge_pass(q, kind):
                op0, op1 = (ALU.min, ALU.max) if kind == MAX else (ALU.mult, ALU.add)

                def filtered(i, k):
                    n, b = i * SLOTS + k, k % 2
                    dve.wait_ge(s_w, n + 1)
                    dve.wait_ge(s_gath[k], 16 * TPC * (i + 1))
                    at_least(dve, s_counted, n)
                    nc.vector.tensor_tensor(edges_of[:], edges_of[:], ps_w[b][:, TPC * D:TPC * D + HIGHS], ALU.add
                                            ).then_inc(s_counted, 1)
                    at_least(dve, s_xt, n - 1)
                    nc.vector.tensor_tensor(msg[b][:], ps_w[b][:, 0:TPC * D], rows[k][:], ALU.mult).then_inc(s_msg, 1)

                def reduce(i, k):
                    n, h, b = i * SLOTS + k, k // CPH, k % 2
                    lo = (k % CPH) * CHUNK
                    dve.wait_ge(s_xt, n + 1)
                    dve.wait_ge(s_flags[h], 16 * (i + 1))
                    at_least(dve, s_back, n + 1 - BUFS)
                    at_least(dve, s_scan, n)
                    nc.vector.tensor_tensor_scan(out=scan[k % BUFS][:], data0=flags[h][:, lo:lo + CHUNK], data1=ps_x[b][0:D, :],
                                                 initial=scan[(k - 1) % BUFS][:, CHUNK - 1:CHUNK], op0=op0, op1=op1
                                                 ).then_inc(s_scan, 1)

                def chunk(i, k, behind):
                    if kind == FILTER:
                        if behind >= 1:
                            filtered(*before(i, k, 1))
                        if behind >= 2:
                            reduce(*before(i, k, 2))
                    else:
                        reduce(i, k)

                first, last = q * ITERS, (q + 1) * ITERS - 1

                def iteration(i, behind):
                    if q == 1:
                        split_layer2(i - q * ITERS)
                    for k in range(SLOTS):
                        if q == 0:
                            one_hot(i, k)
                        chunk(i, k, behind + k)
                    if q == 0:
                        split_layer0(i + AHEAD, 0)

                iteration(first, 0)
                with dve.Fori(first + 1, last + 1) as i:
                    iteration(i, SLOTS)
                if kind == FILTER:
                    filtered(last, SLOTS - 1)
                    reduce(last, SLOTS - 2)
                    reduce(last, SLOTS - 1)

            def masked(ph, g, j, h):
                dve.wait_ge(pair["fetched"][h], 16 * GT * ph.after("fetched", j + 1))
                at_least(dve, step["agg_tr"], ph.after("agg_tr", g - 1))
                nc.vector.tensor_tensor(aggm[h][:], agg[h][:],
                                        mask[:, bass.ds(g * GT, GT)].unsqueeze(2).to_broadcast([P, GT, D]),
                                        ALU.mult).then_inc(step["masked"], 1)

            def conv_phase(ph):
                def one(g, j, h):
                    if within(g):
                        masked(ph, g, j, h)
                    if within(g - 2):
                        dve.wait_ge(step["conv_ev"], ph.after("conv_ev", g - 1))
                        for c in range(2):
                            n0 = (g - 2) * GROUP + c * (GROUP // 2)
                            width = min(GROUP // 2, N - n0) if isinstance(g, int) else GROUP // 2
                            m = nc.vector.bn_stats(conv_stats[:, bass.ds(2 * (g - 2) + c, 1), :].rearrange("d a s -> d (a s)"),
                                                   conv[:, bass.ds(n0, width)])
                        m.then_inc(step["conv_bn"], 1)
                over_groups(dve, one)
                _, _, w, bias, a = ph.conv
                gn_step = iter(range(1, GN_STEPS + 1))

                def gn_after(instruction):
                    instruction.then_inc(step["gn"], 1)
                    dve.wait_ge(step["gn"], ph.after("gn", next(gn_step)))

                dve.wait_ge(step["conv_bn"], ph.after("conv_bn", GROUPS))
                gn_after(nc.vector.bn_aggr(gn_mv[:], conv_stats[:].rearrange("d a s -> d (a s)")))
                gn_after(nc.vector.tensor_tensor(gcol(G_AMEAN), gn_mv[:, 0:1], col(a), ALU.mult))
                gn_after(nc.vector.tensor_tensor(gcol(G_DIFF), gn_mv[:, 0:1], gcol(G_AMEAN), ALU.subtract))
                gn_after(nc.vector.scalar_tensor_tensor(out=gcol(G_VAR), in0=gcol(G_DIFF), scalar=gcol(G_DIFF),
                                                        in1=gn_mv[:, 1:2], op0=ALU.mult, op1=ALU.add))
                dve.wait_ge(step["gn"], ph.after("gn", next(gn_step)))
                gn_after(nc.vector.reciprocal(gcol(G_RSTD), gcol(G_STD)))
                gn_after(nc.vector.tensor_tensor(gcol(G_SCALE), gcol(G_RSTD), col(w), ALU.mult))
                gn_after(nc.vector.tensor_tensor(gcol(G_PROD), gcol(G_AMEAN), gcol(G_SCALE), ALU.mult))
                gn_after(nc.vector.tensor_tensor(gcol(G_SHIFT), col(bias), gcol(G_PROD), ALU.subtract))

            def invert(ph, g, h):
                tiles = bass.ds(g * GT, GT)
                dve.wait_ge(step["std"], ph.after("std", g + 1))
                nc.vector.reciprocal(rstd_all[:, tiles], std[:]).then_inc(step["rstd"], 1)
                dve.wait_ge(step["rstd"], ph.after("rstd", g + 1))
                nc.vector.scalar_tensor_tensor(out=shift_all[:, tiles], in0=mv[h][:, :, 0], scalar=-1.0,
                                               in1=rstd_all[:, tiles], op0=ALU.mult, op1=ALU.mult).then_inc(step["shift"], 1)

            def centred_phase(ph):
                def statistics(g, h):
                    dve.wait_ge(step["z"], ph.after("z", g + 1))
                    at_least(dve, step["mv"], ph.after("mv", g))
                    for t in range(GT):
                        m = nc.vector.bn_stats(stats[:, t, :], ps_z[h][:, t * D:(t + 1) * D])
                    m.then_inc(step["bn"], 1)
                    at_least(dve, step["std"], ph.after("std", g - 1))
                    dve.wait_ge(step["bn"], ph.after("bn", g + 1))
                    settle(dve, s_tally_dve)
                    for t in range(GT):
                        m = nc.vector.bn_aggr(mv[h][:, t, :], stats[:, t, :])
                    m.then_inc(step["mv"], 1)
                    nc.vector.tensor_copy(ph.keep[:, bass.ds(g * GT, GT), :],
                                          ps_z[h][:, 0:GT * D].rearrange("p (t d) -> p t d", t=GT)).then_inc(step["kept"], 1)

                def one(g, j, h):
                    if within(g - 2):
                        invert(ph, g - 2, h)
                    if within(g - 1):
                        statistics(g - 1, (h - 1) % 2)
                    if within(g):
                        dve.wait_ge(step["relu"], ph.after("relu", g + 1))
                        at_least(dve, step["tab"], ph.after("tab", g - 1))
                        settle(dve, s_tally_dve)
                        nc.vector.tensor_tensor(y_t[h][:].rearrange("d (t p) -> d t p", p=P),
                                                relu_t[h][:].rearrange("d (p t) -> d t p", t=GT),
                                                sum_t[:, bass.ds(g * GROUP, GROUP)].rearrange("d (t p) -> d t p", p=P),
                                                ALU.add).then_inc(step["y"], 1)
                over_groups(dve, one)

            def node_phase(ph):
                def chain(g, j, h):
                    now = ps_z[h][:, 0:GT * D].rearrange("p (t d) -> p t d", t=GT)
                    tiles = bass.ds(g * GT, GT)
                    if ph.finish or ph.wn is not None:
                        dve.wait_ge(step["z"], ph.after("z", g + 1))
                    if ph.has_pre:
                        at_least(dve, step[ph.closing], ph.after(ph.closing, g))
                        scale = mask if ph.scale is None else ph.scale
                        if ph.wn is None:
                            dve.wait_ge(pair["fetched"][h], 16 * GT * ph.after("fetched", j + 1))
                        settle(dve, s_tally_dve)
                        for t in range(GT):
                            m = nc.vector.scalar_tensor_tensor(
                                out=z[:, t, :], in0=agg[h][:, t, :] if ph.wn is None else ps_z[h][:, t * D:(t + 1) * D],
                                scalar=scale[:, bass.ds(g * GT + t, 1)],
                                in1=root_all[:, bass.ds(g * GT + t, 1), :].rearrange("p a d -> p (a d)"),
                                op0=ALU.mult, op1=ALU.add)
                        m.then_inc(step["pre"], 1)
                        dve.wait_ge(step["pre"], ph.after("pre", g + 1))
                        now = z[:]
                    if ph.has_u:
                        if ph.norm:
                            at_least(dve, step["y"], ph.after("y", g))
                        target = u[:] if ph.norm else ph.keep[:, tiles, :]
                        if ph.finish:
                            nc.vector.tensor_tensor(target, now, ph.rest[:, tiles, :], ALU.add).then_inc(step["u"], 1)
                        else:
                            m = nc.vector.scalar_tensor_tensor(out=target, in0=now, scalar=0.01, in1=now,
                                                               op0=ALU.mult, op1=ALU.max)
                            if ph.tmat is not None and not ph.norm:
                                at_least(dve, step["new_tr"], ph.after("new_tr", g - 1))
                                m = nc.vector.scalar_tensor_tensor(out=new[h][:], in0=now, scalar=0.01, in1=now,
                                                                   op0=ALU.mult, op1=ALU.max)
                            m.then_inc(step["u"], 1)
                        dve.wait_ge(step["u"], ph.after("u", g + 1))
                        now = u[:]
                    if not ph.norm:
                        return
                    at_least(dve, step["new"], ph.after("new", g - 1))
                    y_moves = ph.keep_step == "y"
                    target = ph.keep[:, tiles, :] if y_moves else y[h][:]
                    if ph.act == "relu":
                        m = nc.vector.scalar_tensor_tensor(out=target, in0=now, scalar=0.0, in1=ph.rest[:, tiles, :],
                                                           op0=ALU.max, op1=ALU.add)
                    else:
                        m = nc.vector.tensor_tensor(target, now, ph.rest[:, tiles, :], ALU.add)
                    m.then_inc(step["y"], 1)
                    dve.wait_ge(step["y"], ph.after("y", g + 1))
                    at_least(dve, step["mv"], ph.after("mv", g))
                    settle(dve, s_tally_dve)
                    for t in range(GT):
                        source = ph.keep[:, bass.ds(g * GT + t, 1), :].rearrange("p a d -> p (a d)") if y_moves else y[h][:, t, :]
                        m = nc.vector.bn_stats(stats[:, t, :], source)
                    m.then_inc(step["bn"], 1)
                    at_least(dve, step["std"], ph.after("std", g - 1))
                    dve.wait_ge(step["bn"], ph.after("bn", g + 1))
                    settle(dve, s_tally_dve)
                    for t in range(GT):
                        m = nc.vector.bn_aggr(mv[h][:, t, :], stats[:, t, :])
                    m.then_inc(step["mv"], 1)
                    invert(ph, g, h)

                def one(g, j, h):
                    if ph.masks and within(g):
                        masked(ph, g, j, h)
                    if within(g - 1):
                        chain(g - 1, *earlier(j, h, 1))
                over_groups(dve, one)

            for b in range(AHEAD):
                split_layer0(b, b)
            make_flags()
            make_digits()
            prepare_weights()
            split_weights()
            for q, kind in enumerate(PASSES):
                if q == 2:
                    for h in range(2):
                        dve.wait_ge(pair["new_out"][h], 16 * f1.after("new_out", PAIRS))
                    nc.vector.tensor_tensor(rows_a[:], rows_a[:], rows_b, ALU.add).then_inc(s_sum, 1)
                edge_pass(q, kind)
                if q == 0:
                    make_counts()
                    make_ends()
                if q == 2:
                    dve.wait_ge(s_sum_ev, NT_ROOM)
                if ROOTS[q] is not None:
                    dve.wait_ge(s_root_out, root_start(q + 1))
                for ph in PHASES[q]:
                    if ph.conv is not None:
                        conv_phase(ph)
                    elif ph.centred:
                        centred_phase(ph)
                    else:
                        node_phase(ph)


def kernel(**inputs):
    import numpy as np
    import concourse.bacc as bacc
    from concourse.bass_utils import run_bass_kernel_spmd

    v = {k: np.asarray(a) for k, a in inputs.items()}

    def rows_to(a, n):
        out = np.zeros((n,) + a.shape[1:], a.dtype)
        out[:a.shape[0]] = a
        return out

    def with_bias(w, b=None):
        out = np.zeros((D + 1, D), np.float32)
        out[:D] = w
        if b is not None:
            out[D] = b
        return out

    mats = np.concatenate([
        with_bias(v["L0_gnn_W2"].T, v["L0_gnn_b2"]), with_bias(v["L0_gnn_Ws"].T, v["L0_gnn_bs"]), with_bias(v["L0_gnn_Wn"].T, v["L0_gnn_bn"]),
        with_bias(v["L1_gnn_W1"]), with_bias(v["L1_gnn_W2"]),
        with_bias(v["L2_gnn_W1_msg"]), with_bias(v["L2_gnn_W1_root"], v["L2_gnn_b1"]),
        with_bias(v["L2_gnn_W2_msg"]), with_bias(v["L2_gnn_W2_root"], v["L2_gnn_b2"]),
        with_bias(v["L3_gnn_W_lin"].T, v["L3_gnn_b_lin"]), with_bias(v["L3_gnn_W_root"].T, v["L3_gnn_b_root"]),
    ], axis=1)
    cols = np.stack([v[n] for n in ("L0_gnn_b1", "L0_gnn_b2", "L1_gnn_b1", "L1_gnn_b2", "L1_gnn_gn1_w", "L1_gnn_gn2_w",
                                    "L1_gnn_gn1_b", "L1_gnn_gn2_b", "L1_gnn_gn1_a", "L1_gnn_gn2_a")], axis=1)
    edge_w = np.concatenate([np.tile(v["L0_gnn_W1"].T, (6, 1))] + [
        rows_to(np.tile(v[n], (PARTS, 1)), STACK0) for n in ("L2_gnn_W1_edge", "L2_gnn_W2_edge")], axis=1)
    part_of = np.repeat(np.eye(PARTS, dtype=np.float32), (3 * ED0, 2 * ED0, ED0), axis=0)

    def by_iteration(a, iterations):
        out = np.zeros((iterations, a.shape[1] * STEP), a.dtype)
        out[:ITERS] = rows_to(a, EP).reshape(ITERS, STEP, -1).transpose(0, 2, 1).reshape(ITERS, -1)
        return out

    src_idx = rows_to(v["src"], EP).reshape(EP // HALF, CPH, P, TPC).transpose(0, 2, 1, 3).reshape(EP // HALF, P, CPH * TPC)
    src_idx = np.concatenate([src_idx, src_idx[:1]])
    dst_shifted = np.full((EP + 1, 1), NP, np.int32)
    dst_shifted[1:E + 1, 0] = v["dst"]
    digits = np.tile(np.concatenate([np.tile(np.arange(n, dtype=np.float32), TPC) for n in (P, HIGHS)]), (P, 1))
    lower = np.triu(np.ones((HIGHS, HIGHS), np.float32), 1)
    arrays = {
        "x": rows_to(v["x"], NP), "mats": mats, "cols": cols, "edge_w": edge_w, "part_of": part_of, "eye": np.eye(P, dtype=np.float32),
        "digits": digits, "lower": lower, "src_idx": src_idx, "dst_shifted": dst_shifted,
        "ea17": by_iteration(v["edge_attr_17"], ITERS + AHEAD), "ea32": by_iteration(v["edge_attr_32"], ITERS),
    }
    arrays = {k: np.ascontiguousarray(a) for k, a in arrays.items()}
    nc = bacc.Bacc("TRN2", target_bir_lowering=False, num_devices=1)
    args = [nc.dram_tensor(k, a.shape, mybir.dt.from_np(a.dtype), kind="ExternalInput").ap() for k, a in arrays.items()]
    out = nc.dram_tensor("out", (NP, D), mybir.dt.float32, kind="ExternalOutput").ap()
    build(nc, *args, out)
    r = run_bass_kernel_spmd(nc, [arrays], core_ids=[0])
    return r.results[0]["out"][:N]
```
